# Optimizing a Trainium2 kernel written in Bass

```python
import numpy as np
import jax
import jax.numpy as jnp

def _softmax(x, axis=-1):
    return jax.nn.softmax(x, axis=axis)

def _gelu(x):
    return jax.nn.gelu(x, approximate=True)

def _silu(x):
    return jax.nn.silu(x)

def _sigmoid(x):
    return jax.nn.sigmoid(x)

def _layernorm(x, axis=-1, eps=1e-05):
    m = jnp.mean(x, axis=axis, keepdims=True)
    v = jnp.var(x, axis=axis, keepdims=True)
    return (x - m) / jnp.sqrt(v + eps)

def _scatter_add(tgt, idx, src, axis=0):
    return tgt.at[idx].add(src)

def _segment_sum(src, seg, n):
    return jax.ops.segment_sum(src, seg, n)
kernel_name = 'mk_recurrent_d1_jaxref_r4_18858b'

def setup_inputs(seed: int=0):
    np.random.seed(seed)
    _w = jnp.asarray

    def _L0_attn_setup():
        import jax, jax.numpy as jnp
        import numpy as np
        ROPE_THETA = 10000.0

        def rope(t, rot_dim):
            S = t.shape[-2]
            half = rot_dim // 2
            inv_freq = 1.0 / ROPE_THETA ** (jnp.arange(0, rot_dim, 2, dtype=jnp.float32) / rot_dim)
            freqs = jnp.arange(S, dtype=jnp.float32)[:, None] * inv_freq[None, :]
            freqs = jnp.repeat(freqs, 2, axis=-1)
            cos, sin = (jnp.cos(freqs), jnp.sin(freqs))
            t_rot, t_pass = (t[..., :rot_dim], t[..., rot_dim:])
            x = t_rot.reshape(*t_rot.shape[:-1], half, 2)
            rh = jnp.stack([-x[..., 1], x[..., 0]], axis=-1).reshape(t_rot.shape)
            t_rot = t_rot * cos + rh * sin
            return jnp.concatenate([t_rot, t_pass], axis=-1)

        def feature_map(x):
            norm = jnp.sqrt(jnp.sum(x * x, axis=-1, keepdims=True))
            return x / jnp.maximum(norm, 1e-12)
        key = jax.random.key(seed)
        kx, kwi, kwo = jax.random.split(key, 3)
        B, S, D = (8, 1024, 512)
        scale = 0.02
        return {'X': jax.random.normal(kx, (B, S, D), dtype=jnp.float32), 'W_in': jax.random.normal(kwi, (3 * D, D), dtype=jnp.float32) * scale, 'b_in': jnp.zeros((3 * D,), dtype=jnp.float32), 'W_out': jax.random.normal(kwo, (D, D), dtype=jnp.float32) * scale, 'b_out': jnp.zeros((D,), dtype=jnp.float32)}
    _L0_attn_in = _L0_attn_setup()

    def _L0_ffn_setup():
        import jax, jax.numpy as jnp
        import numpy as np
        B, S, H, I = (1, 64, 512, 1536)

        def _quantized_matmul(x, w, scale):
            wq = w.astype(jnp.float8_e4m3fn).astype(x.dtype)
            y = jnp.einsum('bsi,io->bso', x, wq)
            return y * scale
        key = jax.random.key(seed)
        ks = jax.random.split(key, 7)
        return {'x': jax.random.normal(ks[0], (B, S, H), dtype=jnp.float32), 'gate_w': jax.random.normal(ks[1], (H, I), dtype=jnp.float32) * 0.02, 'up_w': jax.random.normal(ks[2], (H, I), dtype=jnp.float32) * 0.02, 'down_w': jax.random.normal(ks[3], (I, H), dtype=jnp.float32) * 0.02, 'gate_scale': jax.random.uniform(ks[4], (I,), dtype=jnp.float32, minval=0.5, maxval=1.5), 'up_scale': jax.random.uniform(ks[5], (I,), dtype=jnp.float32, minval=0.5, maxval=1.5), 'down_scale': jax.random.uniform(ks[6], (H,), dtype=jnp.float32, minval=0.5, maxval=1.5)}
    _L0_ffn_in = _L0_ffn_setup()
    _d = {'L0_attn_X': _L0_attn_in['X'], 'L0_attn_W_in': _L0_attn_in['W_in'], 'L0_attn_b_in': _L0_attn_in['b_in'], 'L0_attn_W_out': _L0_attn_in['W_out'], 'L0_attn_b_out': _L0_attn_in['b_out'], 'L0_ffn_gate_w': _L0_ffn_in['gate_w'], 'L0_ffn_up_w': _L0_ffn_in['up_w'], 'L0_ffn_down_w': _L0_ffn_in['down_w'], 'L0_ffn_gate_scale': _L0_ffn_in['gate_scale'], 'L0_ffn_up_scale': _L0_ffn_in['up_scale'], 'L0_ffn_down_scale': _L0_ffn_in['down_scale']}
    _x0 = _d['L0_attn_X']
    _d['L0_attn_X'] = jax.random.normal(jax.random.fold_in(jax.random.key(seed), 1), (2, 1024, 512), dtype=_x0.dtype)
    del _x0
    return _d

def reference(L0_attn_X, L0_attn_W_in, L0_attn_b_in, L0_attn_W_out, L0_attn_b_out, L0_ffn_gate_w, L0_ffn_up_w, L0_ffn_down_w, L0_ffn_gate_scale, L0_ffn_up_scale, L0_ffn_down_scale):

    def _L0_attn_ref(X, W_in, b_in, W_out, b_out):
        import jax, jax.numpy as jnp
        import numpy as np
        ROPE_THETA = 10000.0

        def rope(t, rot_dim):
            S = t.shape[-2]
            half = rot_dim // 2
            inv_freq = 1.0 / ROPE_THETA ** (jnp.arange(0, rot_dim, 2, dtype=jnp.float32) / rot_dim)
            freqs = jnp.arange(S, dtype=jnp.float32)[:, None] * inv_freq[None, :]
            freqs = jnp.repeat(freqs, 2, axis=-1)
            cos, sin = (jnp.cos(freqs), jnp.sin(freqs))
            t_rot, t_pass = (t[..., :rot_dim], t[..., rot_dim:])
            x = t_rot.reshape(*t_rot.shape[:-1], half, 2)
            rh = jnp.stack([-x[..., 1], x[..., 0]], axis=-1).reshape(t_rot.shape)
            t_rot = t_rot * cos + rh * sin
            return jnp.concatenate([t_rot, t_pass], axis=-1)

        def feature_map(x):
            norm = jnp.sqrt(jnp.sum(x * x, axis=-1, keepdims=True))
            return x / jnp.maximum(norm, 1e-12)
        D = X.shape[-1]
        QKV = jnp.einsum('bsd,ed->bse', X, W_in) + b_in
        Q, K, V = jnp.split(QKV, 3, axis=-1)
        rot_dim = D // 2
        Q = rope(Q, rot_dim)
        K = rope(K, rot_dim)
        A = jnp.sum(feature_map(K) * V, axis=-2)
        Y = A[:, None, :] * Q
        Y = jnp.einsum('bsd,ed->bse', Y, W_out) + b_out
        return Y + X

    def _L0_ffn_ref(x, gate_w, up_w, down_w, gate_scale, up_scale, down_scale):
        import jax, jax.numpy as jnp
        import numpy as np
        B, S, H, I = (1, 64, 512, 1536)

        def _quantized_matmul(x, w, scale):
            wq = w.astype(jnp.float8_e4m3fn).astype(x.dtype)
            y = jnp.einsum('bsi,io->bso', x, wq)
            return y * scale
        gate = jax.nn.silu(_quantized_matmul(x, gate_w, gate_scale))
        up = _quantized_matmul(x, up_w, up_scale)
        fuse = gate * up
        return _quantized_matmul(fuse, down_w, down_scale)
    x = L0_attn_X
    xn = _layernorm(x, axis=-1)
    s = _L0_attn_ref(xn, L0_attn_W_in, L0_attn_b_in, L0_attn_W_out, L0_attn_b_out)
    g = _silu(_L0_ffn_ref(xn, L0_ffn_gate_w, L0_ffn_up_w, L0_ffn_down_w, L0_ffn_gate_scale, L0_ffn_up_scale, L0_ffn_down_scale))
    x = x + s * g
    return x

_drawn_inputs = setup_inputs


def setup_inputs(seed=0):
    import zlib

    import numpy as np

    out = dict(_drawn_inputs(seed))
    spreads = {'L0_attn_b_in': (0.0, 0.8), 'L0_attn_b_out': (0.0, 2.0)}
    factors = {'L0_attn_W_in': 3.767,
     'L0_attn_W_out': 3.432,
     'L0_ffn_gate_scale': 3.46,
     'L0_ffn_up_scale': 3.865,
     'L0_ffn_down_scale': 3.898}
    for name, (base, spread) in spreads.items():
        noise = np.random.default_rng([zlib.crc32(name.encode()), seed]).standard_normal(out[name].shape)
        drawn = base * np.exp(spread * noise) if base else spread * noise
        out[name] = jnp.asarray(drawn.astype(out[name].dtype))
    for name, factor in factors.items():
        out[name] = (out[name] * factor).astype(out[name].dtype)
    return out
```

```python
from contextlib import ExitStack

import numpy as np

import concourse.bass as bass
from concourse import mybir

P = 128
B, S, D, I = 2, 1024, 512, 1536
KC = D // P
IB = I // P
CH = 512
NCH = B * S // CH
TPC = CH // P
NT = B * S // P
TPB = S // P
ROT = D // 2
HALF = ROT // 2
IPP = KC
NPI = IB // IPP

F32 = mybir.dt.float32
F16 = mybir.dt.float16
BF16 = mybir.dt.bfloat16
U32 = mybir.dt.uint32
ALU = mybir.AluOpType
ACT = mybir.ActivationFunctionType
AX_X = mybir.AxisListType.X
RMAX = bass.bass_isa.ReduceOp.max

LN_EPS = 1e-5
EXPONENT = 0x7F800000
HALF_BIT = 0x00400000
MAGIC_UP = float(2 ** 20)
MAGIC_MIN = 1.5 * 2.0 ** 14
TINY = 2.0 ** -60

PIECES = ([("k", 0), ("v", 0)] + [(w, n) for n in range(NPI) for w in "gu"]
          + [("d", n) for n in range(NPI)] + [("q", 0), ("o", 0)])
PIECE = {key: n for n, key in enumerate(PIECES)}
QUANT = [key for key in PIECES if key[0] in "gud"]
NRAW = 2

RING_A = ([("gate", 0, i) for i in range(IB)] + [("asum", 0, 0)] + [("q", 0, m) for m in range(KC)]
          + [("gate", 1, i) for i in range(IB)] + [("q", 1, m) for m in range(KC)])
RING_B = ([(w, 0, t) for t in range(TPC) for w in "kv"] + [("up", 0, i) for i in range(IB)]
          + [(w, 1, t) for t in range(TPC) for w in "kv"]
          + [("down", 0, t) for t in range(TPC)] + [("out", 0, t) for t in range(TPC)]
          + [("up", 1, i) for i in range(IB)]
          + [("down", 1, t) for t in range(TPC)] + [("out", 1, t) for t in range(TPC)])
PLACE_A = {key: n for n, key in enumerate(RING_A)}
PLACE_B = {key: n for n, key in enumerate(RING_B)}
NA, NB = 2, 4


def at_a(kind, j, n):
    return (j // 2) * len(RING_A) + PLACE_A[(kind, j % 2, n)]


def at_b(kind, j, n):
    return (j // 2) * len(RING_B) + PLACE_B[(kind, j % 2, n)]


def quant_at(key, k):
    return QUANT.index(key) * KC + k


def build(nc, x, w_in_t, b_qc, b_k, b_v, w_out_t, b_out, gate_w, up_w, down_w, gate_s, up_s, down_s,
          cos_f, sin_f, cos_t, sin_t, out):
    with ExitStack() as ctx:
        def sb(name, shape, dt=F32):
            return ctx.enter_context(nc.sbuf_tensor(name, shape, dt))

        def psum(name, shape, dt=F32):
            return ctx.enter_context(nc.psum_tensor(name, shape, dt))

        def sem(name):
            return ctx.enter_context(nc.semaphore(name))

        wg = sb("wg", [P, KC, I], F16)
        wu = sb("wu", [P, KC, I], F16)
        wd = sb("wd", [P, IB, D], BF16)
        wi_hi = sb("wi_hi", [P, KC, 3 * D], F16)
        wi_lo = sb("wi_lo", [P, KC, 3 * D], F16)
        wo_hi = sb("wo_hi", [P, KC, D], F16)
        wo_lo = sb("wo_lo", [P, KC, D], F16)
        raw = sb("raw", [P, NRAW, KC, D])
        xt_hi = sb("xt_hi", [P, 2, KC, CH], F16)
        xt_lo = sb("xt_lo", [P, 2, KC, CH], F16)
        x_in = sb("x_in", [P, 3, D])
        xn = sb("xn", [P, 2, D])
        xn_hl = sb("xn_hl", [P, 2, 2, D], F16)
        bn6 = sb("bn6", [P, 2, 6])
        mv = sb("mv", [P, NT, 2])
        veps = sb("veps", [P, NT])
        rstd = sb("rstd", [P, NT])
        cosf = sb("cosf", [P, S])
        sinf = sb("sinf", [P, S])
        cost = sb("cost", [P, TPB, HALF])
        sint = sb("sint", [P, TPB, HALF])
        bk_row = sb("bk_row", [P, D])
        bv_row = sb("bv_row", [P, D])
        bo_row = sb("bo_row", [P, D])
        ds_row = sb("ds_row", [P, D])
        kk = sb("kk", [P, 2, D])
        kcos = sb("kcos", [P, 2, HALF])
        ksin = sb("ksin", [P, 2, HALF])
        vv = sb("vv", [P, D])
        ksq = sb("ksq", [P, NT])
        krn = sb("krn", [P, NT])
        kv_sum = sb("kv_sum", [P, D])
        big = sb("big", [P, 2 * IB * CH], F16)
        fu_hi = big[:, 0:IB * CH].rearrange("p (i t) -> p i t", i=IB)
        fu_lo = big[:, IB * CH:2 * IB * CH].rearrange("p (i t) -> p i t", i=IB)
        q32 = big[:, 0:2 * KC * CH].bitcast(F32).rearrange("p (m t) -> p m t", m=KC)
        qtmp = big[:, 8 * CH:14 * CH].bitcast(F32).rearrange("p (m t) -> p m t", m=3)
        y_hi = big[:, 14 * CH:18 * CH].rearrange("p (m t) -> p m t", m=KC)
        y_lo = big[:, 18 * CH:22 * CH].rearrange("p (m t) -> p m t", m=KC)
        silu_g = sb("silu_g", [P, 2, CH])
        fuse = sb("fuse", [P, 2, CH])
        gg = sb("gg", [P, TPC, D])
        yy = sb("yy", [P, 3, D])
        magic = yy
        square = sb("square", [P, D])
        xf = sb("xf", [P, 2, D])
        xb = sb("xb", [P, 2, D])
        msum = xb
        ident = sb("ident", [P, P], F16)
        ones = sb("ones", [P, 1])
        mhalf = sb("mhalf", [P, 1])
        gs = sb("gs", [P, IB])
        ngs = sb("ngs", [P, IB])
        us = sb("us", [P, IB])
        nus = sb("nus", [P, IB])
        bq = sb("bq", [P, KC])
        mx = sb("mx", [P, 24])
        mr = sb("mr", [P, 24])
        pw = sb("pw", [P, 24])
        inv = sb("inv", [P, 16])
        scl = sb("scl", [P, 16])
        asum = sb("asum", [P, 2, KC])
        asc = sb("asc", [P, 2, KC])

        ring_a = [psum(f"ring_a{n}", [P, 512]) for n in range(NA)]
        ring_b = [psum(f"ring_b{n}", [P, 512]) for n in range(NB)]
        turn = [psum(f"turn{n}", [P, 2, KC, P], F16) for n in range(2)]

        x_landed = [sem(f"x_landed{n}") for n in range(3)]
        xf_landed = [sem(f"xf_landed{n}") for n in range(2)]
        raw_landed = [sem(f"raw_landed{n}") for n in range(NRAW)]
        small_landed = sem("small_landed")
        table_t_landed = sem("table_t_landed")
        table_f_landed = sem("table_f_landed")
        out_stored = [sem(f"out_stored{n}") for n in range(3)]
        ident_zero = sem("ident_zero")
        ident_ready = sem("ident_ready")
        consts_ready = sem("consts_ready")
        stats_ready = sem("stats_ready")
        veps_ready = sem("veps_ready")
        rstd_ready = sem("rstd_ready")
        xn_ready = sem("xn_ready")
        xn_hi_ready = sem("xn_hi_ready")
        xn_lo_ready = sem("xn_lo_ready")
        turned = sem("turned")
        xt_ready = sem("xt_ready")
        a_full = sem("a_full")
        b_full = sem("b_full")
        v_ready = sem("v_ready")
        scaled_up = sem("scaled_up")
        rounded = sem("rounded")
        w_hi_ready = sem("w_hi_ready")
        w_lo_ready = sem("w_lo_ready")
        wd_ready = sem("wd_ready")
        part_max = sem("part_max")
        all_max = sem("all_max")
        scale_ready = sem("scale_ready")
        k_rotated = sem("k_rotated")
        k_ready = sem("k_ready")
        ksq_ready = sem("ksq_ready")
        krn_ready = sem("krn_ready")
        kv_ready = sem("kv_ready")
        kv_added = sem("kv_added")
        asum_ready = sem("asum_ready")
        asc_ready = sem("asc_ready")
        silu_ready = sem("silu_ready")
        fuse_ready = sem("fuse_ready")
        fu_hi_ready = sem("fu_hi_ready")
        fu_lo_ready = sem("fu_lo_ready")
        q_ready = sem("q_ready")
        q_rotated = sem("q_rotated")
        y_hi_ready = sem("y_hi_ready")
        y_lo_ready = sem("y_lo_ready")
        down_ready = sem("down_ready")
        g_ready = sem("g_ready")
        xb_ready = sem("xb_ready")
        y_ready = sem("y_ready")
        out_ready = sem("out_ready")
        dve_done = sem("dve_done")
        pool_done = sem("pool_done")

        MAXIMA = [("k", 0, 1), ("v", 1, 1), ("f0", 2, 4), ("f1", 6, 4), ("f2", 10, 4), ("q", 14, 2), ("o", 16, 1),
                  ("a0", 17, 1), ("a1", 18, 1)]
        COL = {name: first for name, first, _ in MAXIMA}
        ORD = {name: n for n, (name, _, _) in enumerate(MAXIMA)}
        SC = {"k": 0, "v": 1, "f0": 2, "f1": 3, "f2": 4, "q": 5, "o": 6, "y0": 7, "y1": 8}

        def raw_of(key):
            return raw[:, PIECE[key] % NRAW, :, :]

        def wait_raw(eng, key):
            eng.wait_ge(raw_landed[PIECE[key] % NRAW], 16 * (PIECE[key] // NRAW + 1))

        def raw_source(key):
            kind, n = key
            if kind in "qkv":
                c = "qkv".index(kind) * D
                return w_in_t[:, c:c + D].rearrange("(k p) e -> p k e", p=P)
            if kind == "o":
                return w_out_t.rearrange("(k p) e -> p k e", p=P)
            if kind == "d":
                return down_w[n * D:(n + 1) * D, :].rearrange("(k p) e -> p k e", p=P)
            src = gate_w if kind == "g" else up_w
            return src[:, n * D:(n + 1) * D].rearrange("(k p) i -> p k i", p=P)

        def split_of(key):
            kind = key[0]
            if kind == "o":
                return wo_hi[:, :, :], wo_lo[:, :, :], 3
            c = "qkv".index(kind) * D
            return wi_hi[:, :, c:c + D], wi_lo[:, :, c:c + D], "kvq".index(kind)

        def wait_converted(eng, key):
            if key in QUANT:
                eng.wait_ge(rounded, quant_at(key, KC - 1) + 1)
            else:
                eng.wait_ge(w_lo_ready, KC * (split_of(key)[2] + 1))

        block = ctx.enter_context(nc.Block())

        @block.sync
        def _(sp):
            def load_x(t):
                if t >= 3:
                    sp.wait_ge(xn_ready, t - 2)
                sp.dma_start(x_in[:, t % 3, :], x[t * P:(t + 1) * P, :]).then_inc(x_landed[t % 3], 16)

            def load_piece(n):
                if n >= NRAW:
                    wait_converted(sp, PIECES[n - NRAW])
                sp.dma_start(raw[:, n % NRAW, :, :], raw_source(PIECES[n])).then_inc(raw_landed[n % NRAW], 16)

            def load_xf(t):
                if t >= 2:
                    sp.wait_ge(out_ready, t - 1)
                sp.dma_start(xf[:, t % 2, :], x[t * P:(t + 1) * P, :]).then_inc(xf_landed[t % 2], 16)

            def store(t):
                sp.wait_ge(out_ready, t + 1)
                sp.dma_start(out[t * P:(t + 1) * P, :], yy[:, t % 3, :]).then_inc(out_stored[t % 3], 16)

            for t in range(3):
                load_x(t)
            for n in range(2):
                load_piece(n)
            load_x(3)
            for n in range(2, 4):
                load_piece(n)
            for t in range(4, 8):
                load_x(t)
                load_piece(t)
            for n in range(8, len(PIECES)):
                load_piece(n)
            load_xf(0)
            load_xf(1)
            for j in range(NCH):
                for t in range(j * TPC, (j + 1) * TPC):
                    if j < NCH - 2:
                        load_x(t + 2 * TPC)
                    store(t)
                    if t + 2 < NT:
                        load_xf(t + 2)
            for n in range(3):
                sp.wait_ge(out_stored[n], 16 * len(range(n, NT, 3)))

        @block.gpsimd
        def _(pool):
            own = [0]

            def done(ins):
                own[0] += 1
                ins.then_inc(pool_done, 1)
                return own[0]

            pool.memset(ident[:, :], 0.0).then_inc(ident_zero, 1)
            pool.memset(ones[:, :], 1.0).then_inc(consts_ready, 1)
            pool.memset(mhalf[:, :], -0.5).then_inc(consts_ready, 1)
            pool.wait_ge(ident_zero, 1)
            pool.affine_select(out=ident[:, :], in_=ident[:, :], compare_op=ALU.not_equal, fill=1.0, base=0,
                               pattern=[[-1, P]], channel_multiplier=1).then_inc(ident_ready, 1)
            pool.wait_ge(consts_ready, 2)

            def rsqrt_var(t):
                pool.wait_ge(stats_ready, t + 1)
                n = done(pool.tensor_scalar(veps[:, t:t + 1], mv[:, t, 1:2], LN_EPS, 1.0, ALU.add, ALU.mult))
                pool.wait_ge(pool_done, n)
                pool.tensor_tensor(rstd[:, t:t + 1], veps[:, t:t + 1], mhalf[:, :], ALU.pow).then_inc(rstd_ready, 1)

            def maximum(name):
                c, n = COL[name], MAXIMA[ORD[name]][2]
                pool.wait_ge(part_max, ORD[name] + 1)
                pool.partition_all_reduce(mr[:, c:c + n], mx[:, c:c + n], P, RMAX).then_inc(all_max, 1)

            def rotate_k(t):
                if t == 0:
                    pool.wait_ge(table_t_landed, 32)
                pool.wait_ge(k_ready, t + 1)
                k = kk[:, t % 2, 0:ROT].rearrange("p (a f) -> p a f", a=2)
                c, s = cost[:, t % TPB, :], sint[:, t % TPB, :]
                for a in range(2):
                    done(pool.tensor_tensor(kcos[:, a, :], k[:, a, :], c, ALU.mult))
                    n = done(pool.tensor_tensor(ksin[:, a, :], k[:, a, :], s, ALU.mult))
                pool.wait_ge(pool_done, n)
                pool.tensor_tensor(k[:, 0, :], kcos[:, 0, :], ksin[:, 1, :], ALU.subtract).then_inc(k_rotated, 1)
                pool.tensor_tensor(k[:, 1, :], kcos[:, 1, :], ksin[:, 0, :], ALU.add).then_inc(k_rotated, 1)

            def norm_k(t):
                pool.wait_ge(ksq_ready, t + 1)
                n = done(pool.tensor_tensor(krn[:, t:t + 1], ksq[:, t:t + 1], mhalf[:, :], ALU.pow))
                pool.wait_ge(pool_done, n)
                pool.tensor_scalar(krn[:, t:t + 1], krn[:, t:t + 1], 1e12, 0.0, ALU.min, ALU.max)\
                    .then_inc(krn_ready, 1)

            def add_kv(t):
                pool.wait_ge(kv_ready, t + 1)
                if t % TPB == 0:
                    if t:
                        pool.wait_ge(a_full, at_a("asum", 0, 0) + 1)
                    pool.tensor_copy(kv_sum[:, :], kk[:, t % 2, :]).then_inc(kv_added, 1)
                else:
                    pool.wait_ge(kv_added, t)
                    pool.tensor_tensor(kv_sum[:, :], kv_sum[:, :], kk[:, t % 2, :], ALU.add).then_inc(kv_added, 1)

            def kv(j):
                for t in range(j * TPC, (j + 1) * TPC):
                    rotate_k(t)
                    norm_k(t)
                    add_kv(t)

            def rotate_q(j):
                if j == 0:
                    pool.wait_ge(table_f_landed, 32)
                c0 = (j % 2) * CH
                c, s = cosf[:, c0:c0 + CH], sinf[:, c0:c0 + CH]
                pool.wait_ge(q_ready, KC * j + 2)
                done(pool.tensor_tensor(qtmp[:, 0, :], q32[:, 0, :], c, ALU.mult))
                done(pool.tensor_tensor(qtmp[:, 1, :], q32[:, 1, :], s, ALU.mult))
                n = done(pool.tensor_tensor(qtmp[:, 2, :], q32[:, 0, :], s, ALU.mult))
                pool.wait_ge(pool_done, n)
                pool.tensor_tensor(q32[:, 0, :], qtmp[:, 0, :], qtmp[:, 1, :], ALU.subtract).then_inc(q_rotated, 1)
                pool.wait_ge(q_rotated, 2 * j + 1)
                n = done(pool.tensor_tensor(qtmp[:, 0, :], q32[:, 1, :], c, ALU.mult))
                pool.wait_ge(pool_done, n)
                pool.tensor_tensor(q32[:, 1, :], qtmp[:, 0, :], qtmp[:, 2, :], ALU.add).then_inc(q_rotated, 1)

            def residual(t):
                if t == 0:
                    pool.wait_ge(small_landed, 16 * 7)
                pool.wait_ge(xf_landed[t % 2], 16 * (t // 2 + 1))
                if t >= 2:
                    pool.wait_ge(y_ready, t - 1)
                n = done(pool.tensor_scalar(xb[:, t % 2, :], xf[:, t % 2, :], mv[:, t, 0:1], rstd[:, t:t + 1],
                                            ALU.subtract, ALU.mult))
                pool.wait_ge(pool_done, n)
                pool.tensor_tensor(xb[:, t % 2, :], xb[:, t % 2, :], bo_row[:, :], ALU.add).then_inc(xb_ready, 1)

            def finish(t):
                pool.wait_ge(y_ready, t + 1)
                pool.wait_ge(g_ready, t + 1)
                n = done(pool.tensor_tensor(yy[:, t % 3, :], yy[:, t % 3, :], gg[:, t % TPC, :], ALU.mult))
                pool.wait_ge(pool_done, n)
                pool.tensor_tensor(yy[:, t % 3, :], yy[:, t % 3, :], xf[:, t % 2, :], ALU.add).then_inc(out_ready, 1)

            for t in range(TPC - 1):
                rsqrt_var(t)
            maximum("k")
            rsqrt_var(TPC - 1)
            maximum("v")
            maximum("f0")
            for j in range(NCH):
                if j % 2 == 0:
                    kv(j)
                if j + 1 < NCH:
                    for t in range((j + 1) * TPC, (j + 2) * TPC):
                        rsqrt_var(t)
                        if j == 0 and t == 5:
                            maximum("f1")
                        if j == 0 and t == 7:
                            maximum("f2")
                if j % 2 == 0:
                    kv(j + 1)
                if j == 0:
                    maximum("q")
                    maximum("o")
                if j % 2 == 0:
                    maximum(f"a{j // 2}")
                rotate_q(j)
                first = j * TPC
                residual(first)
                for t in range(first, first + TPC):
                    if t + 1 < first + TPC:
                        residual(t + 1)
                    finish(t)

        @block.scalar
        def _(act):
            rows = ((bk_row, b_k), (bv_row, b_v), (ds_row, down_s), (bo_row, b_out))
            act.dma_start(gs[:, :], gate_s).then_inc(small_landed, 16)
            act.dma_start(us[:, :], up_s).then_inc(small_landed, 16)
            act.dma_start(bq[:, :], b_qc).then_inc(small_landed, 16)
            for row, src in rows:
                act.dma_start(row[:, :], src.rearrange("(a e) -> a e", a=1).broadcast_to([P, D]))\
                    .then_inc(small_landed, 16)
            act.dma_start(cost[:, :, :], cos_t).then_inc(table_t_landed, 16)
            act.dma_start(sint[:, :, :], sin_t).then_inc(table_t_landed, 16)
            act.dma_start(cosf[:, :], cos_f).then_inc(table_f_landed, 16)
            act.dma_start(sinf[:, :], sin_f).then_inc(table_f_landed, 16)

            def xn_high(t):
                act.wait_ge(xn_ready, t + 1)
                if t >= 2:
                    act.wait_ge(turned, t - 1)
                nc.scalar.activation(xn_hl[:, t % 2, 0, :], xn[:, t % 2, :], ACT.Copy).then_inc(xn_hi_ready, 1)

            def evacuate_turned(t):
                act.wait_ge(turned, t + 1)
                c = (t % TPC) * P
                nc.scalar.activation(xt_hi[:, (t // TPC) % 2, :, c:c + P], turn[t % 2][:, 0, :, :], ACT.Copy)
                nc.scalar.activation(xt_lo[:, (t // TPC) % 2, :, c:c + P], turn[t % 2][:, 1, :, :], ACT.Copy)\
                    .then_inc(xt_ready, 1)

            def norm_step(j, step):
                if 1 <= step < TPC + 1:
                    xn_high(j * TPC + step - 1)
                if 3 <= step < TPC + 3:
                    evacuate_turned(j * TPC + step - 3)

            def scale_up(key, k0, k1):
                wait_raw(act, key)
                for k in range(k0, k1):
                    n = quant_at(key, k)
                    if n >= 3:
                        act.wait_ge(rounded, n - 2)
                    nc.scalar.activation(magic[:, n % 3, :], raw_of(key)[:, k, :], ACT.Copy, scale=MAGIC_UP)\
                        .then_inc(scaled_up, 1)

            def weight_high(key, col):
                hi, _, _ = split_of(key)
                act.wait_ge(scale_ready, col + 1)
                for k in range(KC):
                    nc.scalar.activation(hi[:, k, :], raw_of(key)[:, k, :], ACT.Copy,
                                         scale=scl[:, SC[key[0]]:SC[key[0]] + 1]).then_inc(w_hi_ready, 1)

            def scale_down(n):
                act.wait_ge(rounded, KC * (QUANT.index(("d", n)) + 1))
                nc.scalar.activation(wd[:, n * KC:(n + 1) * KC, :], wd[:, n * KC:(n + 1) * KC, :], ACT.Copy,
                                     scale=inv[:, SC[f"f{n}"]:SC[f"f{n}"] + 1]).then_inc(wd_ready, 1)

            def square_k(t):
                act.wait_ge(k_rotated, 2 * (t + 1))
                if t:
                    act.wait_ge(ksq_ready, t)
                nc.scalar.activation(square[:, :], kk[:, t % 2, :], ACT.Square, accum_out=ksq[:, t:t + 1])\
                    .then_inc(ksq_ready, 1)

            def silu_gate(j, i):
                n = IB * j + i
                act.wait_ge(a_full, at_a("gate", j, i) + 1)
                if n >= 2:
                    act.wait_ge(fuse_ready, n - 1)
                nc.scalar.activation(silu_g[:, n % 2, :], ring_a[at_a("gate", j, i) % NA][:, :], ACT.Silu,
                                     scale=ngs[:, i:i + 1]).then_inc(silu_ready, 1)

            def fuse_high(j, i):
                n = IB * j + i
                act.wait_ge(fuse_ready, n + 1)
                nc.scalar.activation(fu_hi[:, i, :], fuse[:, n % 2, :], ACT.Copy).then_inc(fu_hi_ready, 1)

            def gate_up(j):
                for i in range(IB):
                    silu_gate(j, i)
                    if j == 0 and i < IB - IPP:
                        key = ("gu"[(i % IPP) // 2], i // IPP + 1)
                        scale_up(key, 2 * (i % 2), 2 * (i % 2) + 2)
                    if i:
                        fuse_high(j, i - 1)
                    if j + 1 < NCH and 1 <= i <= TPC + 3:
                        norm_step(j + 1, i - 1)
                fuse_high(j, IB - 1)

            def take_q(j):
                for m in range(KC):
                    a = at_a("q", j, m)
                    act.wait_ge(a_full, a + 1)
                    nc.scalar.activation(q32[:, m, :], ring_a[a % NA][:, :], ACT.Identity, bias=bq[:, m:m + 1],
                                         scale=inv[:, SC["q"]:SC["q"] + 1]).then_inc(q_ready, 1)

            def y_high(j):
                act.wait_ge(asc_ready, j // 2 + 1)
                for m in (2, 3, 0, 1):
                    if m < 2:
                        act.wait_ge(q_rotated, 2 * j + m + 1)
                    else:
                        act.wait_ge(q_ready, KC * j + m + 1)
                    nc.scalar.activation(y_hi[:, m, :], q32[:, m, :], ACT.Copy, scale=asc[:, j // 2, m:m + 1])\
                        .then_inc(y_hi_ready, 1)

            def silu_down(j):
                for t in range(j * TPC, (j + 1) * TPC):
                    act.wait_ge(down_ready, t + 1)
                    nc.scalar.activation(gg[:, t % TPC, :], gg[:, t % TPC, :], ACT.Silu, scale=-1.0)\
                        .then_inc(g_ready, 1)

            for step in range(TPC + 3):
                norm_step(0, step)
                if step == 3:
                    weight_high(("k", 0), ORD["k"])
            weight_high(("v", 0), ORD["v"])
            for j in range(NCH):
                if j % 2 == 0:
                    for t in range(j * TPC, (j + 1) * TPC):
                        if j == 0:
                            key = ("gu"[t // 2], 0)
                            scale_up(key, 2 * (t % 2), 2 * (t % 2) + 2)
                        square_k(t)
                gate_up(j)
                if j % 2 == 0:
                    for t in range((j + 1) * TPC, (j + 2) * TPC):
                        if j == 0 and t < 4 + NPI:
                            scale_up(("d", t - 4), 0, KC)
                            scale_down(t - 4)
                        square_k(t)
                if j == 0:
                    weight_high(("q", 0), ORD["q"])
                    weight_high(("o", 0), ORD["o"])
                silu_down(j)
                if j % 2 == 0:
                    a = at_a("asum", j, 0)
                    act.wait_ge(a_full, a + 1)
                    nc.scalar.activation(asum[:, j // 2, :], ring_a[a % NA][:, 0:KC], ACT.Copy)\
                        .then_inc(asum_ready, 1)
                take_q(j)
                y_high(j)

        @block.vector
        def _(dve):
            own = [0]

            def done(ins):
                own[0] += 1
                ins.then_inc(dve_done, 1)
                return own[0]

            def then(ins):
                dve.wait_ge(dve_done, done(ins))

            def statistics(t):
                dve.wait_ge(x_landed[t % 3], 16 * (t // 3 + 1))
                then(dve.bn_stats(bn6[:, t % 2, :], x_in[:, t % 3, :]))
                dve.bn_aggr(mv[:, t, :], bn6[:, t % 2, :]).then_inc(stats_ready, 1)

            def normalise(t):
                dve.wait_ge(rstd_ready, t + 1)
                dve.wait_ge(stats_ready, t + 1)
                dve.tensor_scalar(xn[:, t % 2, :], x_in[:, t % 3, :], mv[:, t, 0:1], rstd[:, t:t + 1],
                                  ALU.subtract, ALU.mult).then_inc(xn_ready, 1)

            def xn_low(t):
                dve.wait_ge(xn_hi_ready, t + 1)
                dve.tensor_tensor(xn_hl[:, t % 2, 1, :], xn[:, t % 2, :], xn_hl[:, t % 2, 0, :], ALU.subtract)\
                    .then_inc(xn_lo_ready, 1)

            def norm_step(j, step):
                if step < TPC:
                    statistics(j * TPC + step)
                if 2 <= step < TPC + 2:
                    xn_low(j * TPC + step - 2)
                if 1 <= step < TPC + 1:
                    normalise(j * TPC + step - 1)

            def largest(key, col):
                wait_raw(dve, key)
                return dve.tensor_reduce(mx[:, col:col + 1], raw_of(key).rearrange("p k e -> p (k e)"), AX_X,
                                         ALU.max, apply_absolute_value=True)

            def powers(name):
                c, n = COL[name], MAXIMA[ORD[name]][2]
                dve.wait_ge(all_max, ORD[name] + 1)
                then(dve.tensor_scalar(pw[:, c:c + n], mr[:, c:c + n], TINY, None, ALU.max))
                then(dve.tensor_scalar(pw[:, c:c + n].bitcast(U32), pw[:, c:c + n].bitcast(U32), EXPONENT, None,
                                       ALU.bitwise_and))
                return pw[:, c:c + n]

            def set_scale(name, source, factor):
                c = SC[name]
                then(dve.tensor_scalar(inv[:, c:c + 1], source, factor, None, ALU.mult))
                return dve.reciprocal(scl[:, c:c + 1], inv[:, c:c + 1])

            def piece_scale(kind):
                p = powers(kind)
                set_scale(kind, p[:, 0:1], 2.0 ** -14).then_inc(scale_ready, 1)

            def weight_low(key):
                _, lo, n = split_of(key)
                hi, _, _ = split_of(key)
                dve.wait_ge(scale_ready, ORD[key[0]] + 1)
                for k in range(KC):
                    dve.wait_ge(w_hi_ready, KC * n + k + 1)
                    dve.scalar_tensor_tensor(lo[:, k, :], raw_of(key)[:, k, :], scl[:, SC[key[0]]:SC[key[0]] + 1],
                                             hi[:, k, :], ALU.mult, ALU.subtract).then_inc(w_lo_ready, 1)

            def ffn_scale(n):
                c = COL[f"f{n}"]
                powers(f"f{n}")
                then(dve.tensor_tensor(pw[:, c:c + 2], pw[:, c:c + 2], pw[:, c + 2:c + 4], ALU.mult))
                then(dve.tensor_tensor(pw[:, c:c + 1], pw[:, c:c + 1], pw[:, c + 1:c + 2], ALU.mult))
                then(set_scale(f"f{n}", pw[:, c:c + 1], 2.0 ** 7))
                dve.tensor_scalar(nus[:, n * IPP:(n + 1) * IPP], us[:, n * IPP:(n + 1) * IPP],
                                  scl[:, SC[f"f{n}"]:SC[f"f{n}"] + 1], -1.0, ALU.mult, ALU.mult)\
                    .then_inc(scale_ready, 1)

            def small_maxima(n):
                c = COL[f"f{n}"]
                for col, src in ((c + 2, gs), (c + 3, us)):
                    done(dve.tensor_reduce(mx[:, col:col + 1], src[:, n * IPP:(n + 1) * IPP], AX_X, ALU.max,
                                           apply_absolute_value=True))

            def quantised(key, k):
                kind, n = key
                if kind == "d":
                    return wd[:, n * KC + k, :]
                return (wg if kind == "g" else wu)[:, k, n * D:(n + 1) * D]

            def quantise(key, k0, k1):
                wait_raw(dve, key)
                summed = {}
                made = {}
                for step in range(k0, k1 + 2):
                    if k0 <= step - 2:
                        n = quant_at(key, step - 2)
                        dve.wait_ge(dve_done, summed[step - 2])
                        dve.scalar_tensor_tensor(quantised(key, step - 2), magic[:, n % 3, :], MAGIC_MIN,
                                                 msum[:, n % 2, :], ALU.max, ALU.subtract).then_inc(rounded, 1)
                    if step < k1:
                        n = quant_at(key, step)
                        m = magic[:, n % 3, :].bitcast(U32)
                        dve.wait_ge(scaled_up, n + 1)
                        made[step] = done(dve.tensor_scalar(m, m, EXPONENT, HALF_BIT, ALU.bitwise_and,
                                                            ALU.bitwise_or))
                    if k0 <= step - 1 < k1:
                        n = quant_at(key, step - 1)
                        dve.wait_ge(dve_done, made[step - 1])
                        if n >= 2:
                            dve.wait_ge(rounded, n - 1)
                        summed[step - 1] = done(dve.scalar_tensor_tensor(
                            msum[:, n % 2, :], magic[:, n % 3, :], MAGIC_MIN, raw_of(key)[:, step - 1, :],
                            ALU.max, ALU.add))

            def take_k(t):
                j = t // TPC
                n = at_b("k", j, t % TPC)
                dve.wait_ge(b_full, n + 1)
                if t >= 2:
                    dve.wait_ge(kv_added, t - 1)
                dve.scalar_tensor_tensor(kk[:, t % 2, :], ring_b[n % NB][:, :], inv[:, SC["k"]:SC["k"] + 1],
                                         bk_row[:, :], ALU.mult, ALU.add).then_inc(k_ready, 1)

            def take_v(t):
                j = t // TPC
                n = at_b("v", j, t % TPC)
                dve.wait_ge(b_full, n + 1)
                if t:
                    dve.wait_ge(kv_ready, t)
                dve.scalar_tensor_tensor(vv[:, :], ring_b[n % NB][:, :], inv[:, SC["v"]:SC["v"] + 1],
                                         bv_row[:, :], ALU.mult, ALU.add).then_inc(v_ready, 1)

            def times_v(t):
                dve.wait_ge(krn_ready, t + 1)
                dve.wait_ge(v_ready, t + 1)
                dve.scalar_tensor_tensor(kk[:, t % 2, :], kk[:, t % 2, :], krn[:, t:t + 1], vv[:, :],
                                         ALU.mult, ALU.mult).then_inc(kv_ready, 1)

            def fuse_block(j, i):
                n = IB * j + i
                b = at_b("up", j, i)
                dve.wait_ge(b_full, b + 1)
                dve.wait_ge(silu_ready, n + 1)
                if n >= 2:
                    dve.wait_ge(fu_lo_ready, n - 1)
                if j == 0 and i % IPP == 0:
                    dve.wait_ge(scale_ready, ORD[f"f{i // IPP}"] + 1)
                dve.scalar_tensor_tensor(fuse[:, n % 2, :], ring_b[b % NB][:, :], nus[:, i:i + 1],
                                         silu_g[:, n % 2, :], ALU.mult, ALU.mult).then_inc(fuse_ready, 1)

            def fuse_low(j, i):
                n = IB * j + i
                dve.wait_ge(fu_hi_ready, n + 1)
                dve.tensor_tensor(fu_lo[:, i, :], fuse[:, n % 2, :], fu_hi[:, i, :], ALU.subtract)\
                    .then_inc(fu_lo_ready, 1)

            def gate_up(j):
                for i in range(IB):
                    if j == 0 and i == 0:
                        small_maxima(1)
                    if j == 0 and i % IPP == 0 and i // IPP + 1 < NPI:
                        n = i // IPP + 1
                        done(largest(("g", n), COL[f"f{n}"]))
                        largest(("u", n), COL[f"f{n}"] + 1).then_inc(part_max, 1)
                        if n + 1 < NPI:
                            small_maxima(n + 1)
                    if j == 0 and i < IB - IPP:
                        key = ("gu"[(i % IPP) // 2], i // IPP + 1)
                        quantise(key, 2 * (i % 2), 2 * (i % 2) + 2)
                        if i % IPP == 3:
                            ffn_scale(i // IPP + 1)
                    if i:
                        fuse_low(j, i - 1)
                    fuse_block(j, i)
                    if j + 1 < NCH and 1 <= i <= TPC + 3:
                        norm_step(j + 1, i - 1)
                fuse_low(j, IB - 1)

            def take_down(j):
                for t in range(TPC):
                    b = at_b("down", j, t)
                    dve.wait_ge(b_full, b + 1)
                    if j:
                        dve.wait_ge(out_ready, j * TPC - TPC + t + 1)
                    dve.tensor_tensor(gg[:, t, :], ring_b[b % NB][:, :], ds_row[:, :], ALU.mult)\
                        .then_inc(down_ready, 1)

            def scale_a(b):
                c = COL[f"a{b}"]
                dve.wait_ge(asum_ready, b + 1)
                dve.tensor_reduce(mx[:, c:c + 1], asum[:, b, :], AX_X, ALU.max, apply_absolute_value=True)\
                    .then_inc(part_max, 1)
                p = powers(f"a{b}")
                y = SC[f"y{b}"]
                then(dve.tensor_tensor(pw[:, c:c + 1], p, pw[:, COL["q"] + 1:COL["q"] + 2], ALU.mult))
                then(set_scale(f"y{b}", pw[:, c:c + 1], 2.0 ** -13))
                dve.tensor_scalar(asc[:, b, :], asum[:, b, :], scl[:, y:y + 1], None, ALU.mult)\
                    .then_inc(asc_ready, 1)
                then(dve.tensor_tensor(inv[:, y:y + 1], inv[:, y:y + 1], inv[:, SC["o"]:SC["o"] + 1], ALU.mult))

            def y_low(j):
                for n, m in enumerate((2, 3, 0, 1)):
                    dve.wait_ge(y_hi_ready, KC * j + n + 1)
                    dve.scalar_tensor_tensor(y_lo[:, m, :], q32[:, m, :], asc[:, j // 2, m:m + 1], y_hi[:, m, :],
                                             ALU.mult, ALU.subtract).then_inc(y_lo_ready, 1)

            def take_out(j):
                y = SC[f"y{j // 2}"]
                for t in range(j * TPC, (j + 1) * TPC):
                    b = at_b("out", j, t % TPC)
                    dve.wait_ge(b_full, b + 1)
                    dve.wait_ge(xb_ready, t + 1)
                    if t >= 3:
                        dve.wait_ge(out_stored[t % 3], 16 * (t // 3))
                    dve.scalar_tensor_tensor(yy[:, t % 3, :], ring_b[b % NB][:, :], inv[:, y:y + 1],
                                             xb[:, t % 2, :], ALU.mult, ALU.add).then_inc(y_ready, 1)

            def split_piece(kind, col):
                largest((kind, 0), col).then_inc(part_max, 1)
                piece_scale(kind)
                weight_low((kind, 0))

            for step in range(2):
                norm_step(0, step)
            largest(("k", 0), COL["k"]).then_inc(part_max, 1)
            norm_step(0, 2)
            piece_scale("k")
            for step in range(3, TPC + 2):
                norm_step(0, step)
            weight_low(("k", 0))
            dve.wait_ge(small_landed, 16 * 7)
            then(dve.tensor_scalar(ngs[:, :], gs[:, :], -1.0, None, ALU.mult))
            split_piece("v", COL["v"])
            small_maxima(0)
            done(largest(("g", 0), COL["f0"]))
            largest(("u", 0), COL["f0"] + 1).then_inc(part_max, 1)
            ffn_scale(0)
            for j in range(NCH):
                if j % 2 == 0:
                    for t in range(j * TPC, (j + 1) * TPC):
                        take_k(t)
                        if t % TPC:
                            times_v(t - 1)
                        take_v(t)
                        if j == 0:
                            key = ("gu"[t // 2], 0)
                            quantise(key, 2 * (t % 2), 2 * (t % 2) + 2)
                    times_v(t)
                gate_up(j)
                if j % 2 == 0:
                    for t in range((j + 1) * TPC, (j + 2) * TPC):
                        take_k(t)
                        if t % TPC:
                            times_v(t - 1)
                        take_v(t)
                        if j == 0 and t < 4 + NPI:
                            quantise(("d", t - 4), 0, KC)
                    times_v(t)
                if j == 0:
                    done(dve.tensor_reduce(mx[:, COL["q"] + 1:COL["q"] + 2], bq[:, :], AX_X, ALU.max,
                                           apply_absolute_value=True))
                    largest(("q", 0), COL["q"]).then_inc(part_max, 1)
                    powers("q")
                    c = COL["q"]
                    set_scale("q", pw[:, c:c + 1], 2.0 ** -14).then_inc(scale_ready, 1)
                    then(dve.scalar_tensor_tensor(pw[:, c + 1:c + 2], pw[:, c:c + 1], 2.0 * D, mr[:, c + 1:c + 2],
                                                  ALU.mult, ALU.add))
                    then(dve.tensor_scalar(pw[:, c + 1:c + 2].bitcast(U32), pw[:, c + 1:c + 2].bitcast(U32),
                                           EXPONENT, None, ALU.bitwise_and))
                    weight_low(("q", 0))
                    split_piece("o", COL["o"])
                take_down(j)
                if j % 2 == 0:
                    scale_a(j // 2)
                y_low(j)
                take_out(j)

        @block.tensor
        def _(pe):
            def fill_a(kind, j, n):
                a = at_a(kind, j, n)
                if a >= NA:
                    wait_a_free(a - NA)
                return ring_a[a % NA]

            def wait_a_free(a):
                b, n = divmod(a, len(RING_A))
                kind, jj, i = RING_A[n]
                j = 2 * b + jj
                if kind == "gate":
                    pe.wait_ge(silu_ready, IB * j + i + 1)
                elif kind == "q":
                    pe.wait_ge(q_ready, KC * j + i + 1)
                else:
                    pe.wait_ge(asum_ready, b + 1)

            def wait_b_free(b):
                batch, n = divmod(b, len(RING_B))
                kind, jj, i = RING_B[n]
                j = 2 * batch + jj
                if kind == "up":
                    pe.wait_ge(fuse_ready, IB * j + i + 1)
                else:
                    reader = {"k": k_ready, "v": v_ready, "down": down_ready, "out": y_ready}[kind]
                    pe.wait_ge(reader, TPC * j + i + 1)

            def fill_b(kind, j, n):
                b = at_b(kind, j, n)
                if b >= NB:
                    wait_b_free(b - NB)
                return ring_b[b % NB]

            def transposes(t):
                if t == 0:
                    pe.wait_ge(ident_ready, 1)
                pe.wait_ge(xn_lo_ready, t + 1)
                pe.wait_ge(xn_hi_ready, t + 1)
                if t >= 2:
                    pe.wait_ge(xt_ready, t - 1)
                for h in range(2):
                    for k in range(KC):
                        last = pe.transpose(turn[t % 2][:, h, k, :], xn_hl[:, t % 2, h, k * P:(k + 1) * P],
                                            ident[:, :])
                last.then_inc(turned, 1)

            def products(dst, terms):
                for n, (lhs, rhs) in enumerate(terms):
                    last = pe.matmul(dst, lhs, rhs, start=(n == 0), stop=(n == len(terms) - 1))
                return last

            def kv_tile(t):
                j, c = t // TPC, (t % TPC) * P
                pe.wait_ge(xt_ready, t + 1)
                for n, w in enumerate("kv"):
                    dst = fill_b(w, j, t % TPC)
                    if t == 0:
                        wait_converted(pe, (w, 0))
                    e = (1 + n) * D
                    terms = []
                    for k in range(KC):
                        hi, lo = xt_hi[:, j % 2, k, c:c + P], xt_lo[:, j % 2, k, c:c + P]
                        terms += [(hi, wi_hi[:, k, e:e + D]), (hi, wi_lo[:, k, e:e + D]), (lo, wi_hi[:, k, e:e + D])]
                    products(dst[:, :], terms).then_inc(b_full, 1)

            def gate_up(j):
                pe.wait_ge(xt_ready, TPC * (j + 1))
                for i in range(IB):
                    for kind, w, fill, full in (("g", wg, lambda: fill_a("gate", j, i), a_full),
                                                ("u", wu, lambda: fill_b("up", j, i), b_full)):
                        dst = fill()
                        if j == 0 and i % IPP == 0:
                            pe.wait_ge(rounded, quant_at((kind, i // IPP), KC - 1) + 1)
                        terms = []
                        for k in range(KC):
                            wk = w[:, k, i * P:(i + 1) * P]
                            terms += [(wk, xt_hi[:, j % 2, k, :]), (wk, xt_lo[:, j % 2, k, :])]
                        products(dst[:, :], terms).then_inc(full, 1)
                    if j + 1 < NCH and 4 <= i < 4 + TPC:
                        transposes((j + 1) * TPC + i - 4)

            def down(j):
                pe.wait_ge(fu_lo_ready, IB * (j + 1))
                pe.wait_ge(fu_hi_ready, IB * (j + 1))
                if j == 0:
                    pe.wait_ge(wd_ready, NPI)
                for t in range(TPC):
                    dst = fill_b("down", j, t)
                    c = t * P
                    terms = []
                    for i in range(IB):
                        terms += [(fu_hi[:, i, c:c + P], wd[:, i, :]), (fu_lo[:, i, c:c + P], wd[:, i, :])]
                    products(dst[:, :], terms).then_inc(b_full, 1)

            def sum_tokens(b):
                dst = fill_a("asum", 2 * b, 0)
                pe.wait_ge(kv_added, TPB * (b + 1))
                pe.wait_ge(consts_ready, 2)
                for m in range(KC):
                    last = pe.matmul(dst[:, m:m + 1], kv_sum[:, m * P:(m + 1) * P], ones[:, :], start=True, stop=True)
                last.then_inc(a_full, 1)

            def queries(j):
                if j == 0:
                    wait_converted(pe, ("q", 0))
                for m in range(KC):
                    dst = fill_a("q", j, m)
                    terms = []
                    for k in range(KC):
                        hi, lo = wi_hi[:, k, m * P:(m + 1) * P], wi_lo[:, k, m * P:(m + 1) * P]
                        terms += [(hi, xt_hi[:, j % 2, k, :]), (hi, xt_lo[:, j % 2, k, :]), (lo, xt_hi[:, j % 2, k, :])]
                    products(dst[:, :], terms).then_inc(a_full, 1)

            def output(j):
                if j == 0:
                    wait_converted(pe, ("o", 0))
                pe.wait_ge(y_lo_ready, KC * (j + 1))
                pe.wait_ge(y_hi_ready, KC * (j + 1))
                for t in range(TPC):
                    dst = fill_b("out", j, t)
                    c = t * P
                    terms = []
                    for m in (2, 3, 0, 1):
                        hi, lo = y_hi[:, m, c:c + P], y_lo[:, m, c:c + P]
                        terms += [(hi, wo_hi[:, m, :]), (hi, wo_lo[:, m, :]), (lo, wo_hi[:, m, :])]
                    products(dst[:, :], terms).then_inc(b_full, 1)

            for t in range(TPC):
                transposes(t)
            for j in range(NCH):
                if j % 2 == 0:
                    for t in range(j * TPC, (j + 1) * TPC):
                        kv_tile(t)
                gate_up(j)
                if j % 2 == 0:
                    for t in range((j + 1) * TPC, (j + 2) * TPC):
                        kv_tile(t)
                down(j)
                if j % 2 == 0:
                    sum_tokens(j // 2)
                queries(j)
                output(j)


def rotation_tables():
    inv_freq = (1.0 / (10000.0 ** (np.arange(0, ROT, 2, dtype=np.float64) / ROT))).astype(np.float32)
    angle = (np.arange(S, dtype=np.float32)[:, None] * inv_freq[None, :]).astype(np.float64)
    return np.cos(angle).astype(np.float32), np.sin(angle).astype(np.float32)


def kernel(L0_attn_X, L0_attn_W_in, L0_attn_b_in, L0_attn_W_out, L0_attn_b_out, L0_ffn_gate_w, L0_ffn_up_w,
           L0_ffn_down_w, L0_ffn_gate_scale, L0_ffn_up_scale, L0_ffn_down_scale):
    import concourse.bacc as bacc
    from concourse.bass_utils import run_bass_kernel_spmd

    c = np.ascontiguousarray
    order = np.concatenate([np.arange(0, ROT, 2), np.arange(1, ROT, 2), np.arange(ROT, D)])
    order3 = np.concatenate([order, D + order, 2 * D + order])
    b_in = np.asarray(L0_attn_b_in)[order3]
    cos, sin = rotation_tables()
    arrays = {
        "x": c(np.asarray(L0_attn_X).reshape(B * S, D)),
        "w_in_t": c(np.asarray(L0_attn_W_in)[order3].T),
        "b_qc": c(b_in[0:D].reshape(KC, P).T),
        "b_k": c(b_in[D:2 * D]),
        "b_v": c(b_in[2 * D:3 * D]),
        "w_out_t": c(np.asarray(L0_attn_W_out).T[order]),
        "b_out": c(np.asarray(L0_attn_b_out)),
        "gate_w": c(np.asarray(L0_ffn_gate_w)),
        "up_w": c(np.asarray(L0_ffn_up_w)),
        "down_w": c(np.asarray(L0_ffn_down_w)),
        "gate_s": c(np.asarray(L0_ffn_gate_scale).reshape(IB, P).T),
        "up_s": c(np.asarray(L0_ffn_up_scale).reshape(IB, P).T),
        "down_s": c(np.asarray(L0_ffn_down_scale)),
        "cos_f": c(cos.T),
        "sin_f": c(sin.T),
        "cos_t": c(cos.reshape(TPB, P, HALF).transpose(1, 0, 2)),
        "sin_t": c(sin.reshape(TPB, P, HALF).transpose(1, 0, 2)),
    }
    nc = bacc.Bacc("TRN2", target_bir_lowering=False, num_devices=1)
    args = [nc.dram_tensor(n, a.shape, mybir.dt.from_np(a.dtype), kind="ExternalInput").ap() for n, a in arrays.items()]
    args.append(nc.dram_tensor("out", (B * S, D), F32, kind="ExternalOutput").ap())
    build(nc, *args)
    r = run_bass_kernel_spmd(nc, [arrays], core_ids=[0])
    return r.results[0]["out"].reshape(B, S, D)
```

```python
from contextlib import ExitStack

import numpy as np

import concourse.bass as bass
from concourse import mybir

P = 128
B, S, D, I = 2, 1024, 512, 1536
KC = D // P
IB = I // P
CH = 512
NCH = B * S // CH
TPC = CH // P
NT = B * S // P
TPB = S // P
ROT = D // 2
HALF = ROT // 2
IPP = KC
NPI = IB // IPP

F32 = mybir.dt.float32
F16 = mybir.dt.float16
BF16 = mybir.dt.bfloat16
U32 = mybir.dt.uint32
ALU = mybir.AluOpType
ACT = mybir.ActivationFunctionType
AX_X = mybir.AxisListType.X
RMAX = bass.bass_isa.ReduceOp.max
RADD = bass.bass_isa.ReduceOp.add

LN_EPS = 1e-5
EXPONENT = 0x7F800000
HALF_BIT = 0x00400000
MAGIC_UP = float(2 ** 20)
MAGIC_MIN = 1.5 * 2.0 ** 14
TINY = 2.0 ** -60
F16_MAX = 65504.0

PIECES = ([("k", 0), ("v", 0)] + [(w, n) for n in range(NPI) for w in "gu"]
          + [("q", 0)] + [("d", n) for n in range(NPI)] + [("o", 0)])
PIECE = {key: n for n, key in enumerate(PIECES)}
QUANT = [key for key in PIECES if key[0] in "gud"]
NRAW = 3

RING_A = ([("gate", 0, i) for i in range(IB)] + [("q", 0, m) for m in range(KC)] + [("asum", 0, 0)]
          + [("gate", 1, i) for i in range(IB)] + [("q", 1, m) for m in range(KC)])
RING_B = ([(w, 0, t) for t in range(TPC) for w in "kv"] + [("up", 0, i) for i in range(IB)]
          + [(w, 1, t) for t in range(TPC) for w in "kv"]
          + [("down", 0, t) for t in range(TPC)] + [("out", 0, t) for t in range(TPC)]
          + [("up", 1, i) for i in range(IB)]
          + [("down", 1, t) for t in range(TPC)] + [("out", 1, t) for t in range(TPC)])
PLACE_A = {key: n for n, key in enumerate(RING_A)}
PLACE_B = {key: n for n, key in enumerate(RING_B)}
NA, NB = 2, 4


def at_a(kind, j, n):
    return (j // 2) * len(RING_A) + PLACE_A[(kind, j % 2, n)]


def at_b(kind, j, n):
    return (j // 2) * len(RING_B) + PLACE_B[(kind, j % 2, n)]


def quant_at(key, k):
    return QUANT.index(key) * KC + k


def build(nc, x, w_in_t, b_qc, b_k, b_v, w_out_t, b_out, gate_w, up_w, down_w, gate_s, up_s, down_s,
          cos_f, sin_f, cos_t, sin_t, out):
    with ExitStack() as ctx:
        def sb(name, shape, dt=F32):
            return ctx.enter_context(nc.sbuf_tensor(name, shape, dt))

        def psum(name, shape, dt=F32):
            return ctx.enter_context(nc.psum_tensor(name, shape, dt))

        def sem(name):
            return ctx.enter_context(nc.semaphore(name))

        wg = sb("wg", [P, KC, I], F16)
        wu = sb("wu", [P, KC, I], F16)
        wd = sb("wd", [P, IB, D], BF16)
        wi_hi = sb("wi_hi", [P, KC, 3 * D], F16)
        wi_lo = sb("wi_lo", [P, KC, 3 * D], F16)
        wo_hi = sb("wo_hi", [P, KC, D], F16)
        wo_lo = sb("wo_lo", [P, KC, D], F16)
        raw = sb("raw", [P, NRAW, KC, D])
        q32 = raw[:, 1, :, :]
        qtmp = raw[:, 2, 0:3, :]
        gg = raw[:, 2, :, :]
        xt_hi = sb("xt_hi", [P, 2, KC, CH], F16)
        xt_lo = sb("xt_lo", [P, 2, KC, CH], F16)
        x_in = sb("x_in", [P, 4, D])
        xn = sb("xn", [P, 2, D])
        xn_hl = sb("xn_hl", [P, 2, 2, D], F16)
        bn6 = sb("bn6", [P, 2, 6])
        mv = sb("mv", [P, NT, 2])
        veps = sb("veps", [P, NT])
        rstd = sb("rstd", [P, NT])
        shift = sb("shift", [P, NT])
        cosf = sb("cosf", [P, S])
        sinf = sb("sinf", [P, S])
        cost = sb("cost", [P, TPB, HALF])
        sint = sb("sint", [P, TPB, HALF])
        bk_row = sb("bk_row", [P, D])
        bv_row = sb("bv_row", [P, D])
        bo_row = sb("bo_row", [P, D])
        ds_row = sb("ds_row", [P, D])
        kv_or_y = sb("kv_or_y", [P, 4, D])
        kk = kv_or_y[:, 0:2, :]
        vv = kv_or_y[:, 2, :]
        square = kv_or_y[:, 3, :]
        y_halves = kv_or_y[:, :, :].rearrange("p a e -> p (a e)").bitcast(F16)
        y_hi = y_halves[:, 0:KC * CH].rearrange("p (m t) -> p m t", m=KC)
        y_lo = y_halves[:, KC * CH:2 * KC * CH].rearrange("p (m t) -> p m t", m=KC)
        kcos = sb("kcos", [P, 2, HALF])
        ksin = sb("ksin", [P, 2, HALF])
        ksq = sb("ksq", [P, NT])
        krn = sb("krn", [P, NT])
        kv_sum = sb("kv_sum", [P, D])
        fu_hi = sb("fu_hi", [P, IB, CH], F16)
        fu_lo = sb("fu_lo", [P, IB, CH], F16)
        silu_g = sb("silu_g", [P, 2, CH])
        fuse = sb("fuse", [P, 2, CH])
        yy = sb("yy", [P, 3, D])
        magic = yy
        xf = sb("xf", [P, 2, D])
        xb = sb("xb", [P, 2, D])
        msum = xb
        ident = sb("ident", [P, P], F16)
        ones = sb("ones", [P, 1])
        mhalf = sb("mhalf", [P, 2])
        gs = sb("gs", [P, IB])
        ngs = sb("ngs", [P, IB])
        us = sb("us", [P, IB])
        nus = sb("nus", [P, IB])
        bq = sb("bq", [P, KC])
        ssq = sb("ssq", [P, 13, KC])
        ssqp = sb("ssqp", [P, 13])
        norm2 = sb("norm2", [P, 13])
        rnorm = sb("rnorm", [P, 13])
        mx = sb("mx", [P, 8])
        mr = sb("mr", [P, 8])
        room = sb("room", [P, 2])
        qmax = sb("qmax", [P, 2])
        inv = sb("inv", [P, 16])
        scl = sb("scl", [P, 16])
        asum = sb("asum", [P, 2, KC])
        asc = sb("asc", [P, 2, KC])

        ring_a = [psum(f"ring_a{n}", [P, 512]) for n in range(NA)]
        ring_b = [psum(f"ring_b{n}", [P, 512]) for n in range(NB)]
        turn = [psum(f"turn{n}", [P, 2, KC, P], F16) for n in range(2)]

        x_landed = [sem(f"x_landed{n}") for n in range(4)]
        xf_landed = [sem(f"xf_landed{n}") for n in range(2)]
        raw_landed = [sem(f"raw_landed{n}") for n in range(NRAW)]
        small_landed = sem("small_landed")
        table_t_landed = sem("table_t_landed")
        table_f_landed = sem("table_f_landed")
        out_stored = [sem(f"out_stored{n}") for n in range(3)]
        ident_zero = sem("ident_zero")
        ident_ready = sem("ident_ready")
        consts_ready = sem("consts_ready")
        stats_ready = sem("stats_ready")
        veps_ready = sem("veps_ready")
        rstd_ready = sem("rstd_ready")
        xn_ready = sem("xn_ready")
        xn_hi_ready = sem("xn_hi_ready")
        xn_lo_ready = sem("xn_lo_ready")
        turned = sem("turned")
        xt_ready = sem("xt_ready")
        a_full = sem("a_full")
        b_full = sem("b_full")
        v_ready = sem("v_ready")
        scaled_up = sem("scaled_up")
        rounded = sem("rounded")
        w_hi_ready = sem("w_hi_ready")
        w_lo_ready = sem("w_lo_ready")
        wd_ready = sem("wd_ready")
        squares_ready = sem("squares_ready")
        ssqp_ready = sem("ssqp_ready")
        rnorm_ready = sem("rnorm_ready")
        part_max = sem("part_max")
        all_max = sem("all_max")
        x_shifted = sem("x_shifted")
        scale_ready = sem("scale_ready")
        k_rotated = sem("k_rotated")
        k_ready = sem("k_ready")
        ksq_ready = sem("ksq_ready")
        krn_ready = sem("krn_ready")
        kv_ready = sem("kv_ready")
        kv_added = sem("kv_added")
        asum_ready = sem("asum_ready")
        asc_ready = sem("asc_ready")
        silu_ready = sem("silu_ready")
        fuse_ready = sem("fuse_ready")
        fu_hi_ready = sem("fu_hi_ready")
        fu_lo_ready = sem("fu_lo_ready")
        q_ready = sem("q_ready")
        q_rotated = sem("q_rotated")
        y_hi_ready = sem("y_hi_ready")
        y_lo_ready = sem("y_lo_ready")
        down_ready = sem("down_ready")
        g_ready = sem("g_ready")
        xb_ready = sem("xb_ready")
        y_ready = sem("y_ready")
        yg_ready = sem("yg_ready")
        out_ready = sem("out_ready")
        dve_done = sem("dve_done")
        pool_done = sem("pool_done")

        NORMS = [("k", [("k", 0)]), ("v", [("v", 0)])] + [(f"f{n}", [("g", n), ("u", n)]) for n in range(NPI)] \
            + [("q", [("q", 0)]), ("o", [("o", 0)])]
        ORD = {name: n for n, (name, _) in enumerate(NORMS)}
        MAXIMA = [("scales", 0, 3), ("a0", 3, 1), ("a1", 4, 1)]
        COL = {name: first for name, first, _ in MAXIMA}
        MORD = {name: n for n, (name, _, _) in enumerate(MAXIMA)}
        SC = {"k": 0, "v": 1, "f0": 2, "f1": 3, "f2": 4, "q": 5, "o": 6, "y0": 7, "y1": 8}

        SUMMED = [key for _, pieces in NORMS for key in pieces]

        def raw_of(key):
            return raw[:, PIECE[key] % NRAW, :, :]

        def wait_raw(eng, key):
            eng.wait_ge(raw_landed[PIECE[key] % NRAW], 16 * (PIECE[key] // NRAW + 1))

        def raw_source(key):
            kind, n = key
            if kind in "qkv":
                c = "qkv".index(kind) * D
                return w_in_t[:, c:c + D].rearrange("(k p) e -> p k e", p=P)
            if kind == "o":
                return w_out_t.rearrange("(k p) e -> p k e", p=P)
            if kind == "d":
                return down_w[n * D:(n + 1) * D, :].rearrange("(k p) e -> p k e", p=P)
            src = gate_w if kind == "g" else up_w
            return src[:, n * D:(n + 1) * D].rearrange("(k p) i -> p k i", p=P)

        def split_of(key):
            kind = key[0]
            if kind == "o":
                return wo_hi[:, :, :], wo_lo[:, :, :], 3
            c = "qkv".index(kind) * D
            return wi_hi[:, :, c:c + D], wi_lo[:, :, c:c + D], "kvq".index(kind)

        def wait_converted(eng, key):
            if key in QUANT:
                eng.wait_ge(rounded, quant_at(key, KC - 1) + 1)
            else:
                eng.wait_ge(w_lo_ready, KC * (split_of(key)[2] + 1))

        block = ctx.enter_context(nc.Block())

        @block.sync
        def _(sp):
            def load_x(t):
                if t >= 4:
                    sp.wait_ge(xn_ready, t - 3)
                sp.dma_start(x_in[:, t % 4, :], x[t * P:(t + 1) * P, :]).then_inc(x_landed[t % 4], 16)

            def load_piece(n):
                if n >= NRAW:
                    wait_converted(sp, PIECES[n - NRAW])
                sp.dma_start(raw[:, n % NRAW, :, :], raw_source(PIECES[n])).then_inc(raw_landed[n % NRAW], 16)

            def load_xf(t):
                if t >= 2:
                    sp.wait_ge(out_ready, t - 1)
                sp.dma_start(xf[:, t % 2, :], x[t * P:(t + 1) * P, :]).then_inc(xf_landed[t % 2], 16)

            def store(t):
                sp.wait_ge(out_ready, t + 1)
                sp.dma_start(out[t * P:(t + 1) * P, :], yy[:, t % 3, :]).then_inc(out_stored[t % 3], 16)

            for t in range(4):
                load_x(t)
            load_piece(0)
            load_piece(1)
            load_piece(2)
            for dst, src in ((gs, gate_s), (us, up_s), (bq, b_qc)):
                sp.dma_start(dst[:, :], src).then_inc(small_landed, 16)
            for row, src in ((bk_row, b_k), (bv_row, b_v), (ds_row, down_s), (bo_row, b_out)):
                sp.dma_start(row[:, :], src.rearrange("(a e) -> a e", a=1).broadcast_to([P, D]))\
                    .then_inc(small_landed, 16)
            sp.dma_start(cost[:, :, :], cos_t).then_inc(table_t_landed, 16)
            sp.dma_start(sint[:, :, :], sin_t).then_inc(table_t_landed, 16)
            for t in range(4, 8):
                load_x(t)
            for n in range(3, 9):
                load_piece(n)
            sp.dma_start(cosf[:, :], cos_f).then_inc(table_f_landed, 16)
            sp.dma_start(sinf[:, :], sin_f).then_inc(table_f_landed, 16)
            for n in range(9, len(PIECES)):
                load_piece(n)
            load_xf(0)
            load_xf(1)
            for j in range(NCH):
                for t in range(j * TPC, (j + 1) * TPC):
                    if j < NCH - 2:
                        load_x(t + 2 * TPC)
                    store(t)
                    if t + 2 < NT:
                        load_xf(t + 2)
            for n in range(3):
                sp.wait_ge(out_stored[n], 16 * len(range(n, NT, 3)))

        @block.gpsimd
        def _(pool):
            own = [0]

            def done(ins):
                own[0] += 1
                ins.then_inc(pool_done, 1)
                return own[0]

            pool.memset(ident[:, :], 0.0).then_inc(ident_zero, 1)
            pool.memset(ones[:, :], 1.0).then_inc(consts_ready, 1)
            pool.memset(mhalf[:, :], -0.5).then_inc(consts_ready, 1)
            pool.wait_ge(ident_zero, 1)
            pool.affine_select(out=ident[:, :], in_=ident[:, :], compare_op=ALU.not_equal, fill=1.0, base=0,
                               pattern=[[-1, P]], channel_multiplier=1).then_inc(ident_ready, 1)
            pool.wait_ge(consts_ready, 2)

            def rsqrt_var(t):
                pool.wait_ge(stats_ready, t + 1)
                n = done(pool.tensor_scalar(veps[:, t:t + 1], mv[:, t, 1:2], LN_EPS, 1.0, ALU.add, ALU.mult))
                pool.wait_ge(pool_done, n)
                pool.tensor_tensor(rstd[:, t:t + 1], veps[:, t:t + 1], mhalf[:, 0:1], ALU.pow).then_inc(rstd_ready, 1)

            def xn_low(t):
                pool.wait_ge(xn_hi_ready, t + 1)
                pool.tensor_tensor(xn_hl[:, t % 2, 1, :], xn[:, t % 2, :], xn_hl[:, t % 2, 0, :], ALU.subtract)\
                    .then_inc(xn_lo_ready, 1)
                pool.wait_ge(rstd_ready, t + 1)
                done(pool.tensor_scalar(shift[:, t:t + 1], mv[:, t, 0:1], rstd[:, t:t + 1], -1.0, ALU.mult, ALU.mult))

            def norm_step(j, step):
                if step < TPC:
                    rsqrt_var(j * TPC + step)
                if 1 <= step:
                    xn_low(j * TPC + step - 1)

            def norms(name):
                pieces = NORMS[ORD[name]][1]
                c, n = PIECE[pieces[0]], len(pieces)
                cols = slice(c, c + n)
                pool.wait_ge(ssqp_ready, ORD[name] + 1)
                m = done(pool.partition_all_reduce(norm2[:, cols], ssqp[:, cols], P, RADD))
                pool.wait_ge(pool_done, m)
                more = (1.25, 3.0) if n == 2 else (1.0, TINY)
                m = done(pool.tensor_scalar(norm2[:, cols], norm2[:, cols], more[0], more[1], ALU.mult, ALU.add))
                pool.wait_ge(pool_done, m)
                pool.tensor_tensor(rnorm[:, cols], norm2[:, cols], mhalf[:, 0:n], ALU.pow).then_inc(rnorm_ready, 1)

            def maximum(name):
                c, n = COL[name], MAXIMA[MORD[name]][2]
                pool.wait_ge(part_max, MORD[name] + 1)
                pool.partition_all_reduce(mr[:, c:c + n], mx[:, c:c + n], P, RMAX).then_inc(all_max, 1)

            def rotate_k(t):
                if t == 0:
                    pool.wait_ge(table_t_landed, 32)
                else:
                    pool.wait_ge(k_rotated, 2 * t)
                pool.wait_ge(k_ready, t + 1)
                k = kk[:, t % 2, 0:ROT].rearrange("p (a f) -> p a f", a=2)
                c, s = cost[:, t % TPB, :], sint[:, t % TPB, :]
                for a in range(2):
                    done(pool.tensor_tensor(kcos[:, a, :], k[:, a, :], c, ALU.mult))
                    n = done(pool.tensor_tensor(ksin[:, a, :], k[:, a, :], s, ALU.mult))
                norm_k(t)
                pool.wait_ge(pool_done, n)
                pool.tensor_tensor(k[:, 0, :], kcos[:, 0, :], ksin[:, 1, :], ALU.subtract).then_inc(k_rotated, 1)
                pool.tensor_tensor(k[:, 1, :], kcos[:, 1, :], ksin[:, 0, :], ALU.add).then_inc(k_rotated, 1)

            def norm_k(t):
                pool.wait_ge(ksq_ready, t + 1)
                n = done(pool.tensor_tensor(krn[:, t:t + 1], ksq[:, t:t + 1], mhalf[:, 0:1], ALU.pow))
                pool.wait_ge(pool_done, n)
                pool.tensor_scalar(krn[:, t:t + 1], krn[:, t:t + 1], 1e12, 0.0, ALU.min, ALU.max)\
                    .then_inc(krn_ready, 1)

            def add_kv(t):
                pool.wait_ge(kv_ready, t + 1)
                if t % TPB == 0:
                    if t:
                        pool.wait_ge(a_full, at_a("asum", 0, 0) + 1)
                    pool.tensor_copy(kv_sum[:, :], kk[:, t % 2, :]).then_inc(kv_added, 1)
                else:
                    pool.wait_ge(kv_added, t)
                    pool.tensor_tensor(kv_sum[:, :], kv_sum[:, :], kk[:, t % 2, :], ALU.add).then_inc(kv_added, 1)

            def kv(j):
                for t in range(j * TPC, (j + 1) * TPC):
                    rotate_k(t)
                    if t % TPC:
                        add_kv(t - 1)
                add_kv(t)

            def rotate_q(j):
                if j == 0:
                    pool.wait_ge(table_f_landed, 32)
                    wait_converted(pool, ("d", NPI - 1))
                c0 = (j % 2) * CH
                c, s = cosf[:, c0:c0 + CH], sinf[:, c0:c0 + CH]
                pool.wait_ge(q_ready, KC * j + 2)
                done(pool.tensor_tensor(qtmp[:, 0, :], q32[:, 0, :], c, ALU.mult))
                done(pool.tensor_tensor(qtmp[:, 1, :], q32[:, 1, :], s, ALU.mult))
                n = done(pool.tensor_tensor(qtmp[:, 2, :], q32[:, 0, :], s, ALU.mult))
                pool.wait_ge(pool_done, n)
                pool.tensor_tensor(q32[:, 0, :], qtmp[:, 0, :], qtmp[:, 1, :], ALU.subtract).then_inc(q_rotated, 1)
                pool.wait_ge(q_rotated, 2 * j + 1)
                n = done(pool.tensor_tensor(qtmp[:, 0, :], q32[:, 1, :], c, ALU.mult))
                pool.wait_ge(pool_done, n)
                pool.tensor_tensor(q32[:, 1, :], qtmp[:, 0, :], qtmp[:, 2, :], ALU.add).then_inc(q_rotated, 1)

            def residual(t):
                if t == 0:
                    pool.wait_ge(small_landed, 16 * 7)
                pool.wait_ge(x_shifted, t + 1)
                pool.tensor_tensor(xb[:, t % 2, :], xb[:, t % 2, :], bo_row[:, :], ALU.add).then_inc(xb_ready, 1)

            def finish(t):
                pool.wait_ge(yg_ready, t + 1)
                pool.tensor_tensor(yy[:, t % 3, :], yy[:, t % 3, :], xf[:, t % 2, :], ALU.add).then_inc(out_ready, 1)

            def fuse_low(j, i):
                n = IB * j + i
                pool.wait_ge(fuse_ready, n + 1)
                pool.wait_ge(fu_hi_ready, n + 1)
                pool.tensor_tensor(fu_lo[:, i, :], fuse[:, n % 2, :], fu_hi[:, i, :], ALU.subtract)\
                    .then_inc(fu_lo_ready, 1)

            for step in range(TPC + 1):
                norm_step(0, step)
            norms("k")
            norms("v")
            for j in range(NCH):
                if j % 2 == 0:
                    kv(j)
                if j == 0:
                    maximum("scales")
                    norms("f0")
                for i in range(IB):
                    if j == 0 and i:
                        fuse_low(j, i - 1)
                    if j + 1 < NCH and i < TPC + 1:
                        norm_step(j + 1, i)
                    if j == 0 and i == 2:
                        norms("f1")
                    if j == 0 and i == 6:
                        norms("f2")
                if j == 0:
                    fuse_low(j, IB - 1)
                    norms("q")
                if j % 2 == 0:
                    kv(j + 1)
                if j == 0:
                    norms("o")
                rotate_q(j)
                if j % 2 == 0:
                    maximum(f"a{j // 2}")
                first = j * TPC
                residual(first)
                residual(first + 1)
                for t in range(first, first + TPC):
                    finish(t)
                    if t + 2 < first + TPC:
                        residual(t + 2)

        @block.scalar
        def _(act):
            def xn_high(t):
                act.wait_ge(xn_ready, t + 1)
                if t >= 2:
                    act.wait_ge(turned, t - 1)
                nc.scalar.activation(xn_hl[:, t % 2, 0, :], xn[:, t % 2, :], ACT.Copy).then_inc(xn_hi_ready, 1)

            def evacuate_turned(t):
                act.wait_ge(turned, t + 1)
                c = (t % TPC) * P
                nc.scalar.activation(xt_hi[:, (t // TPC) % 2, :, c:c + P], turn[t % 2][:, 0, :, :], ACT.Copy)
                nc.scalar.activation(xt_lo[:, (t // TPC) % 2, :, c:c + P], turn[t % 2][:, 1, :, :], ACT.Copy)\
                    .then_inc(xt_ready, 1)

            def sum_squares(key):
                wait_raw(act, key)
                kind, n = key
                if kind in "gu":
                    dst = (wg if kind == "g" else wu)[:, :, n * D:(n + 1) * D]
                else:
                    dst = split_of(key)[0]
                for k in range(KC):
                    nc.scalar.activation(dst[:, k, :], raw_of(key)[:, k, :], ACT.Square,
                                         accum_out=ssq[:, PIECE[key], k:k + 1]).then_inc(squares_ready, 1)

            def scale_up(key, k0, k1):
                wait_raw(act, key)
                for k in range(k0, k1):
                    n = quant_at(key, k)
                    if n >= 3:
                        act.wait_ge(rounded, n - 2)
                    nc.scalar.activation(magic[:, n % 3, :], raw_of(key)[:, k, :], ACT.Copy, scale=MAGIC_UP)\
                        .then_inc(scaled_up, 1)

            def weight_high(key, col):
                hi, _, _ = split_of(key)
                act.wait_ge(scale_ready, col + 1)
                act.wait_ge(squares_ready, KC * (SUMMED.index(key) + 1))
                for k in range(KC):
                    nc.scalar.activation(hi[:, k, :], raw_of(key)[:, k, :], ACT.Copy,
                                         scale=scl[:, SC[key[0]]:SC[key[0]] + 1]).then_inc(w_hi_ready, 1)

            def scale_down(n):
                act.wait_ge(rounded, KC * (QUANT.index(("d", n)) + 1))
                nc.scalar.activation(wd[:, n * KC:(n + 1) * KC, :], wd[:, n * KC:(n + 1) * KC, :], ACT.Copy,
                                     scale=inv[:, SC[f"f{n}"]:SC[f"f{n}"] + 1]).then_inc(wd_ready, 1)

            def square_k(t):
                act.wait_ge(k_ready, t + 1)
                if t:
                    act.wait_ge(ksq_ready, t)
                nc.scalar.activation(square[:, :], kk[:, t % 2, :], ACT.Square, accum_out=ksq[:, t:t + 1])\
                    .then_inc(ksq_ready, 1)

            def silu_gate(j, i):
                n = IB * j + i
                act.wait_ge(a_full, at_a("gate", j, i) + 1)
                if n >= 2:
                    act.wait_ge(fuse_ready, n - 1)
                nc.scalar.activation(silu_g[:, n % 2, :], ring_a[at_a("gate", j, i) % NA][:, :], ACT.Silu,
                                     scale=ngs[:, i:i + 1]).then_inc(silu_ready, 1)

            def fuse_high(j, i):
                n = IB * j + i
                act.wait_ge(fuse_ready, n + 1)
                nc.scalar.activation(fu_hi[:, i, :], fuse[:, n % 2, :], ACT.Copy).then_inc(fu_hi_ready, 1)

            def gate_up(j):
                for i in range(IB):
                    silu_gate(j, i)
                    if i:
                        fuse_high(j, i - 1)
                    if j == 0 and i < IB - IPP:
                        key = ("gu"[(i % IPP) // 2], i // IPP + 1)
                        if i % IPP == 0:
                            sum_squares(key)
                        if i % IPP == 1:
                            sum_squares(("u", key[1]))
                        scale_up(key, 2 * (i % 2), 2 * (i % 2) + 2)
                    if j + 1 < NCH:
                        if 2 <= i < 2 + TPC:
                            xn_high((j + 1) * TPC + i - 2)
                        if 6 <= i < 6 + TPC:
                            evacuate_turned((j + 1) * TPC + i - 6)
                fuse_high(j, IB - 1)

            def shift_x(t):
                act.wait_ge(xf_landed[t % 2], 16 * (t // 2 + 1))
                if t >= 2:
                    act.wait_ge(y_ready, t - 1)
                nc.scalar.activation(xb[:, t % 2, :], xf[:, t % 2, :], ACT.Identity, bias=shift[:, t:t + 1],
                                     scale=rstd[:, t:t + 1]).then_inc(x_shifted, 1)

            def take_q(j):
                if j == 0:
                    wait_converted(act, ("d", 1))
                for m in range(KC):
                    a = at_a("q", j, m)
                    act.wait_ge(a_full, a + 1)
                    nc.scalar.activation(q32[:, m, :], ring_a[a % NA][:, :], ACT.Identity, bias=bq[:, m:m + 1],
                                         scale=inv[:, SC["q"]:SC["q"] + 1]).then_inc(q_ready, 1)

            def y_high(j):
                act.wait_ge(asc_ready, j // 2 + 1)
                for m in (2, 3, 0, 1):
                    if m < 2:
                        act.wait_ge(q_rotated, 2 * j + m + 1)
                    else:
                        act.wait_ge(q_ready, KC * j + m + 1)
                    nc.scalar.activation(y_hi[:, m, :], q32[:, m, :], ACT.Copy, scale=asc[:, j // 2, m:m + 1])\
                        .then_inc(y_hi_ready, 1)

            def silu_down(j):
                for t in range(j * TPC, (j + 1) * TPC):
                    act.wait_ge(down_ready, t + 1)
                    nc.scalar.activation(gg[:, t % TPC, :], gg[:, t % TPC, :], ACT.Silu, scale=-1.0)\
                        .then_inc(g_ready, 1)

            xn_high(0)
            xn_high(1)
            evacuate_turned(0)
            xn_high(2)
            sum_squares(("k", 0))
            evacuate_turned(1)
            xn_high(3)
            evacuate_turned(2)
            sum_squares(("v", 0))
            evacuate_turned(3)
            weight_high(("k", 0), ORD["k"])
            weight_high(("v", 0), ORD["v"])
            scale_up(("g", 0), 0, 2)
            for j in range(NCH):
                if j % 2 == 0:
                    for t in range(j * TPC, (j + 1) * TPC):
                        square_k(t)
                        if j == 0:
                            if t < 2:
                                sum_squares(("gu"[t], 0))
                            if t < 3:
                                key = ("gu"[(t + 1) // 2], 0)
                                scale_up(key, 2 * ((t + 1) % 2), 2 * ((t + 1) % 2) + 2)
                gate_up(j)
                if j % 2 == 0:
                    for t in range((j + 1) * TPC, (j + 2) * TPC):
                        square_k(t)
                        if j == 0:
                            if t == TPC:
                                sum_squares(("q", 0))
                                weight_high(("q", 0), ORD["q"])
                            else:
                                scale_up(("d", t - TPC - 1), 0, KC)
                                scale_down(t - TPC - 1)
                if j == 0:
                    sum_squares(("o", 0))
                    weight_high(("o", 0), ORD["o"])
                take_q(j)
                if j % 2 == 0:
                    a = at_a("asum", j, 0)
                    act.wait_ge(a_full, a + 1)
                    nc.scalar.activation(asum[:, j // 2, :], ring_a[a % NA][:, 0:KC], ACT.Copy)\
                        .then_inc(asum_ready, 1)
                y_high(j)
                for t in range(2):
                    shift_x(j * TPC + t)
                silu_down(j)
                for t in range(2, TPC):
                    shift_x(j * TPC + t)

        @block.vector
        def _(dve):
            own = [0]

            def done(ins):
                own[0] += 1
                ins.then_inc(dve_done, 1)
                return own[0]

            def then(ins):
                dve.wait_ge(dve_done, done(ins))

            def statistics(t):
                dve.wait_ge(x_landed[t % 4], 16 * (t // 4 + 1))
                then(dve.bn_stats(bn6[:, t % 2, :], x_in[:, t % 4, :]))
                dve.bn_aggr(mv[:, t, :], bn6[:, t % 2, :]).then_inc(stats_ready, 1)

            def normalise(t):
                dve.wait_ge(rstd_ready, t + 1)
                dve.wait_ge(stats_ready, t + 1)
                if t >= 2:
                    dve.wait_ge(xn_lo_ready, t - 1)
                dve.tensor_scalar(xn[:, t % 2, :], x_in[:, t % 4, :], mv[:, t, 0:1], rstd[:, t:t + 1],
                                  ALU.subtract, ALU.mult).then_inc(xn_ready, 1)

            def norm_step(j, step):
                if step < TPC:
                    statistics(j * TPC + step)
                if 1 <= step < TPC + 1:
                    normalise(j * TPC + step - 1)

            def add_squares(name):
                pieces = NORMS[ORD[name]][1]
                c, n = PIECE[pieces[0]], len(pieces)
                dve.wait_ge(squares_ready, KC * (SUMMED.index(pieces[-1]) + 1))
                dve.tensor_reduce(ssqp[:, c:c + n], ssq[:, c:c + n, :], AX_X, ALU.add).then_inc(ssqp_ready, 1)

            def power_of(ap):
                then(dve.tensor_scalar(ap.bitcast(U32), ap.bitcast(U32), EXPONENT, None, ALU.bitwise_and))

            def piece_scale(kind):
                c, r = SC[kind], rnorm[:, PIECE[(kind, 0)]:PIECE[(kind, 0)] + 1]
                dve.wait_ge(rnorm_ready, ORD[kind] + 1)
                power_of(r)
                then(dve.tensor_scalar(scl[:, c:c + 1], r, 2.0 ** 15, None, ALU.mult))
                dve.reciprocal(inv[:, c:c + 1], scl[:, c:c + 1]).then_inc(scale_ready, 1)

            def weight_low(key):
                _, lo, n = split_of(key)
                hi, _, _ = split_of(key)
                dve.wait_ge(scale_ready, ORD[key[0]] + 1)
                for k in range(KC):
                    dve.wait_ge(w_hi_ready, KC * n + k + 1)
                    dve.scalar_tensor_tensor(lo[:, k, :], raw_of(key)[:, k, :], scl[:, SC[key[0]]:SC[key[0]] + 1],
                                             hi[:, k, :], ALU.mult, ALU.subtract).then_inc(w_lo_ready, 1)

            def small_maxima():
                for c, src in enumerate((gs, us, bq)):
                    ins = dve.tensor_reduce(mx[:, c:c + 1], src[:, :], AX_X, ALU.max, apply_absolute_value=True)
                    if c < 2:
                        done(ins)
                dve.wait_ge(dve_done, own[0])
                ins.then_inc(part_max, 1)

            def ffn_room():
                dve.wait_ge(all_max, MORD["scales"] + 1)
                then(dve.tensor_tensor(room[:, 0:1], mr[:, 0:1], mr[:, 1:2], ALU.mult))
                then(dve.tensor_scalar(room[:, 0:1], room[:, 0:1], TINY, D / (F16_MAX * 0.99), ALU.max, ALU.mult))
                then(dve.reciprocal(room[:, 1:2], room[:, 0:1]))

            def ffn_scale(n):
                c, r = SC[f"f{n}"], PIECE[("g", n)]
                dve.wait_ge(rnorm_ready, ORD[f"f{n}"] + 1)
                then(dve.scalar_tensor_tensor(scl[:, c:c + 1], rnorm[:, r:r + 1], room[:, 1:2], rnorm[:, r + 1:r + 2],
                                              ALU.mult, ALU.mult))
                power_of(scl[:, c:c + 1])
                then(dve.reciprocal(inv[:, c:c + 1], scl[:, c:c + 1]))
                dve.tensor_scalar(nus[:, n * IPP:(n + 1) * IPP], us[:, n * IPP:(n + 1) * IPP],
                                  scl[:, c:c + 1], -1.0, ALU.mult, ALU.mult).then_inc(scale_ready, 1)

            def quantised(key, k):
                kind, n = key
                if kind == "d":
                    return wd[:, n * KC + k, :]
                return (wg if kind == "g" else wu)[:, k, n * D:(n + 1) * D]

            def quantise(key, k0, k1):
                wait_raw(dve, key)
                if key[0] in "gu":
                    dve.wait_ge(squares_ready, KC * (SUMMED.index(key) + 1))
                summed = {}
                made = {}
                for step in range(k0, k1 + 2):
                    if k0 <= step - 2:
                        n = quant_at(key, step - 2)
                        dve.wait_ge(dve_done, summed[step - 2])
                        dve.scalar_tensor_tensor(quantised(key, step - 2), magic[:, n % 3, :], MAGIC_MIN,
                                                 msum[:, n % 2, :], ALU.max, ALU.subtract).then_inc(rounded, 1)
                    if step < k1:
                        n = quant_at(key, step)
                        m = magic[:, n % 3, :].bitcast(U32)
                        dve.wait_ge(scaled_up, n + 1)
                        made[step] = done(dve.tensor_scalar(m, m, EXPONENT, HALF_BIT, ALU.bitwise_and,
                                                            ALU.bitwise_or))
                    if k0 <= step - 1 < k1:
                        n = quant_at(key, step - 1)
                        dve.wait_ge(dve_done, made[step - 1])
                        if n >= 2:
                            dve.wait_ge(rounded, n - 1)
                        summed[step - 1] = done(dve.scalar_tensor_tensor(
                            msum[:, n % 2, :], magic[:, n % 3, :], MAGIC_MIN, raw_of(key)[:, step - 1, :],
                            ALU.max, ALU.add))

            def take_k(t):
                j = t // TPC
                n = at_b("k", j, t % TPC)
                dve.wait_ge(b_full, n + 1)
                if t >= 2:
                    dve.wait_ge(kv_added, t - 1)
                dve.scalar_tensor_tensor(kk[:, t % 2, :], ring_b[n % NB][:, :], inv[:, SC["k"]:SC["k"] + 1],
                                         bk_row[:, :], ALU.mult, ALU.add).then_inc(k_ready, 1)

            def take_v(t):
                j = t // TPC
                n = at_b("v", j, t % TPC)
                dve.wait_ge(b_full, n + 1)
                if t:
                    dve.wait_ge(kv_ready, t)
                dve.scalar_tensor_tensor(vv[:, :], ring_b[n % NB][:, :], inv[:, SC["v"]:SC["v"] + 1],
                                         bv_row[:, :], ALU.mult, ALU.add).then_inc(v_ready, 1)

            def times_v(t):
                dve.wait_ge(krn_ready, t + 1)
                dve.wait_ge(k_rotated, 2 * (t + 1))
                dve.wait_ge(v_ready, t + 1)
                dve.scalar_tensor_tensor(kk[:, t % 2, :], kk[:, t % 2, :], krn[:, t:t + 1], vv[:, :],
                                         ALU.mult, ALU.mult).then_inc(kv_ready, 1)

            def fuse_block(j, i):
                n = IB * j + i
                b = at_b("up", j, i)
                dve.wait_ge(b_full, b + 1)
                dve.wait_ge(silu_ready, n + 1)
                if n >= 2:
                    dve.wait_ge(fu_lo_ready, n - 1)
                if j == 0 and i % IPP == 0:
                    dve.wait_ge(scale_ready, ORD[f"f{i // IPP}"] + 1)
                dve.scalar_tensor_tensor(fuse[:, n % 2, :], ring_b[b % NB][:, :], nus[:, i:i + 1],
                                         silu_g[:, n % 2, :], ALU.mult, ALU.mult).then_inc(fuse_ready, 1)

            def fuse_low(j, i):
                n = IB * j + i
                dve.wait_ge(fu_hi_ready, n + 1)
                dve.tensor_tensor(fu_lo[:, i, :], fuse[:, n % 2, :], fu_hi[:, i, :], ALU.subtract)\
                    .then_inc(fu_lo_ready, 1)

            def gate_up(j):
                for i in range(IB):
                    if j and i:
                        fuse_low(j, i - 1)
                    fuse_block(j, i)
                    if j == 0 and i < IB - IPP:
                        key = ("gu"[(i % IPP) // 2], i // IPP + 1)
                        quantise(key, 2 * (i % 2), 2 * (i % 2) + 2)
                        if i % IPP == 1:
                            add_squares(f"f{key[1]}")
                        if i % IPP == 3:
                            ffn_scale(key[1])
                    if j + 1 < NCH and i < TPC + 1:
                        norm_step(j + 1, i)
                if j:
                    fuse_low(j, IB - 1)

            def take_down(j):
                for t in range(TPC):
                    b = at_b("down", j, t)
                    dve.wait_ge(b_full, b + 1)
                    if j:
                        dve.wait_ge(out_ready, j * TPC - TPC + t + 1)
                    dve.tensor_tensor(gg[:, t, :], ring_b[b % NB][:, :], ds_row[:, :], ALU.mult)\
                        .then_inc(down_ready, 1)

            def scale_a(b):
                c, y = COL[f"a{b}"], SC[f"y{b}"]
                dve.wait_ge(asum_ready, b + 1)
                dve.tensor_reduce(mx[:, c:c + 1], asum[:, b, :], AX_X, ALU.max, apply_absolute_value=True)\
                    .then_inc(part_max, 1)
                dve.wait_ge(all_max, MORD[f"a{b}"] + 1)
                then(dve.tensor_scalar(mr[:, c:c + 1], mr[:, c:c + 1], TINY, qmax[:, 1:2], ALU.max, ALU.mult))
                then(dve.reciprocal(scl[:, y:y + 1], mr[:, c:c + 1]))
                power_of(scl[:, y:y + 1])
                dve.tensor_scalar(asc[:, b, :], asum[:, b, :], scl[:, y:y + 1], None, ALU.mult)\
                    .then_inc(asc_ready, 1)
                then(dve.reciprocal(inv[:, y:y + 1], scl[:, y:y + 1]))
                then(dve.tensor_tensor(inv[:, y:y + 1], inv[:, y:y + 1], inv[:, SC["o"]:SC["o"] + 1], ALU.mult))

            def q_bound():
                c = SC["q"]
                dve.wait_ge(scale_ready, ORD["q"] + 1)
                then(dve.tensor_scalar(qmax[:, 0:1], inv[:, c:c + 1], 32.0, TINY, ALU.mult, ALU.add))
                then(dve.scalar_tensor_tensor(qmax[:, 1:2], mr[:, 2:3], 2.0 ** -14, qmax[:, 0:1],
                                              ALU.mult, ALU.add))

            def y_low(j):
                for n, m in enumerate((2, 3, 0, 1)):
                    dve.wait_ge(y_hi_ready, KC * j + n + 1)
                    dve.scalar_tensor_tensor(y_lo[:, m, :], q32[:, m, :], asc[:, j // 2, m:m + 1], y_hi[:, m, :],
                                             ALU.mult, ALU.subtract).then_inc(y_lo_ready, 1)

            def take_out(j):
                y = SC[f"y{j // 2}"]
                for t in range(j * TPC, (j + 1) * TPC):
                    b = at_b("out", j, t % TPC)
                    dve.wait_ge(b_full, b + 1)
                    dve.wait_ge(xb_ready, t + 1)
                    if t >= 3:
                        dve.wait_ge(out_stored[t % 3], 16 * (t // 3))
                    dve.scalar_tensor_tensor(yy[:, t % 3, :], ring_b[b % NB][:, :], inv[:, y:y + 1],
                                             xb[:, t % 2, :], ALU.mult, ALU.add).then_inc(y_ready, 1)
                    dve.wait_ge(y_ready, t + 1)
                    dve.wait_ge(g_ready, t + 1)
                    dve.tensor_tensor(yy[:, t % 3, :], yy[:, t % 3, :], gg[:, t % TPC, :], ALU.mult)\
                        .then_inc(yg_ready, 1)

            for step in range(TPC + 1):
                norm_step(0, step)
            add_squares("k")
            piece_scale("k")
            add_squares("v")
            weight_low(("k", 0))
            piece_scale("v")
            weight_low(("v", 0))
            dve.wait_ge(small_landed, 16 * 7)
            small_maxima()
            then(dve.tensor_scalar(ngs[:, :], gs[:, :], -1.0, None, ALU.mult))
            for j in range(NCH):
                if j % 2 == 0:
                    for t in range(j * TPC, (j + 1) * TPC):
                        take_k(t)
                        if j == 0:
                            key = ("gu"[t // 2], 0)
                            quantise(key, 2 * (t % 2), 2 * (t % 2) + 2)
                        if t % TPC:
                            times_v(t - 1)
                        take_v(t)
                    times_v(t)
                if j == 0:
                    add_squares("f0")
                    ffn_room()
                    ffn_scale(0)
                gate_up(j)
                if j % 2 == 0:
                    for t in range((j + 1) * TPC, (j + 2) * TPC):
                        take_k(t)
                        if j == 0:
                            if t == TPC:
                                add_squares("q")
                                piece_scale("q")
                                q_bound()
                                weight_low(("q", 0))
                            else:
                                quantise(("d", t - TPC - 1), 0, KC)
                        if t % TPC:
                            times_v(t - 1)
                        take_v(t)
                    times_v(t)
                if j == 0:
                    add_squares("o")
                    piece_scale("o")
                    weight_low(("o", 0))
                if j % 2 == 0:
                    scale_a(j // 2)
                y_low(j)
                take_down(j)
                take_out(j)

        @block.tensor
        def _(pe):
            def fill_a(kind, j, n):
                a = at_a(kind, j, n)
                if a >= NA:
                    wait_a_free(a - NA)
                return ring_a[a % NA]

            def wait_a_free(a):
                b, n = divmod(a, len(RING_A))
                kind, jj, i = RING_A[n]
                j = 2 * b + jj
                if kind == "gate":
                    pe.wait_ge(silu_ready, IB * j + i + 1)
                elif kind == "q":
                    pe.wait_ge(q_ready, KC * j + i + 1)
                else:
                    pe.wait_ge(asum_ready, b + 1)

            def wait_b_free(b):
                batch, n = divmod(b, len(RING_B))
                kind, jj, i = RING_B[n]
                j = 2 * batch + jj
                if kind == "up":
                    pe.wait_ge(fuse_ready, IB * j + i + 1)
                else:
                    reader = {"k": k_ready, "v": v_ready, "down": down_ready, "out": y_ready}[kind]
                    pe.wait_ge(reader, TPC * j + i + 1)

            def fill_b(kind, j, n):
                b = at_b(kind, j, n)
                if b >= NB:
                    wait_b_free(b - NB)
                return ring_b[b % NB]

            def transposes(t):
                if t == 0:
                    pe.wait_ge(ident_ready, 1)
                pe.wait_ge(xn_lo_ready, t + 1)
                pe.wait_ge(xn_hi_ready, t + 1)
                if t >= 2:
                    pe.wait_ge(xt_ready, t - 1)
                for h in range(2):
                    for k in range(KC):
                        last = pe.transpose(turn[t % 2][:, h, k, :], xn_hl[:, t % 2, h, k * P:(k + 1) * P],
                                            ident[:, :])
                last.then_inc(turned, 1)

            def products(dst, terms):
                for n, (lhs, rhs) in enumerate(terms):
                    last = pe.matmul(dst, lhs, rhs, start=(n == 0), stop=(n == len(terms) - 1))
                return last

            def kv_tile(t):
                j, c = t // TPC, (t % TPC) * P
                pe.wait_ge(xt_ready, t + 1)
                for n, w in enumerate("kv"):
                    dst = fill_b(w, j, t % TPC)
                    if t == 0:
                        wait_converted(pe, (w, 0))
                    e = (1 + n) * D
                    terms = []
                    for k in range(KC):
                        hi, lo = xt_hi[:, j % 2, k, c:c + P], xt_lo[:, j % 2, k, c:c + P]
                        terms += [(hi, wi_hi[:, k, e:e + D]), (hi, wi_lo[:, k, e:e + D]), (lo, wi_hi[:, k, e:e + D])]
                    products(dst[:, :], terms).then_inc(b_full, 1)

            def gate_up(j):
                pe.wait_ge(xt_ready, TPC * (j + 1))
                for i in range(IB):
                    for kind, w, fill, full in (("g", wg, lambda: fill_a("gate", j, i), a_full),
                                                ("u", wu, lambda: fill_b("up", j, i), b_full)):
                        dst = fill()
                        if j == 0 and i % IPP == 0:
                            pe.wait_ge(rounded, quant_at((kind, i // IPP), KC - 1) + 1)
                        terms = []
                        for k in range(KC):
                            wk = w[:, k, i * P:(i + 1) * P]
                            terms += [(wk, xt_hi[:, j % 2, k, :]), (wk, xt_lo[:, j % 2, k, :])]
                        products(dst[:, :], terms).then_inc(full, 1)
                    if j + 1 < NCH and 5 <= i < 5 + TPC:
                        transposes((j + 1) * TPC + i - 5)

            def down(j):
                pe.wait_ge(fu_lo_ready, IB * (j + 1))
                pe.wait_ge(fu_hi_ready, IB * (j + 1))
                if j == 0:
                    pe.wait_ge(wd_ready, NPI)
                for t in range(TPC):
                    dst = fill_b("down", j, t)
                    c = t * P
                    terms = []
                    for i in range(IB):
                        terms += [(fu_hi[:, i, c:c + P], wd[:, i, :]), (fu_lo[:, i, c:c + P], wd[:, i, :])]
                    products(dst[:, :], terms).then_inc(b_full, 1)

            def sum_tokens(b):
                dst = fill_a("asum", 2 * b, 0)
                pe.wait_ge(kv_added, TPB * (b + 1))
                pe.wait_ge(consts_ready, 2)
                for m in range(KC):
                    last = pe.matmul(dst[:, m:m + 1], kv_sum[:, m * P:(m + 1) * P], ones[:, :], start=True, stop=True)
                last.then_inc(a_full, 1)

            def queries(j):
                if j == 0:
                    wait_converted(pe, ("q", 0))
                for m in range(KC):
                    dst = fill_a("q", j, m)
                    terms = []
                    for k in range(KC):
                        hi, lo = wi_hi[:, k, m * P:(m + 1) * P], wi_lo[:, k, m * P:(m + 1) * P]
                        terms += [(hi, xt_hi[:, j % 2, k, :]), (hi, xt_lo[:, j % 2, k, :]), (lo, xt_hi[:, j % 2, k, :])]
                    products(dst[:, :], terms).then_inc(a_full, 1)

            def output(j):
                if j == 0:
                    wait_converted(pe, ("o", 0))
                pe.wait_ge(y_lo_ready, KC * (j + 1))
                pe.wait_ge(y_hi_ready, KC * (j + 1))
                for t in range(TPC):
                    dst = fill_b("out", j, t)
                    c = t * P
                    terms = []
                    for m in (2, 3, 0, 1):
                        hi, lo = y_hi[:, m, c:c + P], y_lo[:, m, c:c + P]
                        terms += [(hi, wo_hi[:, m, :]), (hi, wo_lo[:, m, :]), (lo, wo_hi[:, m, :])]
                    products(dst[:, :], terms).then_inc(b_full, 1)

            for t in range(TPC):
                transposes(t)
            for j in range(NCH):
                if j % 2 == 0:
                    for t in range(j * TPC, (j + 1) * TPC):
                        kv_tile(t)
                gate_up(j)
                if j % 2 == 0:
                    for t in range((j + 1) * TPC, (j + 2) * TPC):
                        kv_tile(t)
                queries(j)
                if j % 2 == 0:
                    sum_tokens(j // 2)
                down(j)
                output(j)


def rotation_tables():
    inv_freq = (1.0 / (10000.0 ** (np.arange(0, ROT, 2, dtype=np.float64) / ROT))).astype(np.float32)
    angle = (np.arange(S, dtype=np.float32)[:, None] * inv_freq[None, :]).astype(np.float64)
    return np.cos(angle).astype(np.float32), np.sin(angle).astype(np.float32)


def kernel(L0_attn_X, L0_attn_W_in, L0_attn_b_in, L0_attn_W_out, L0_attn_b_out, L0_ffn_gate_w, L0_ffn_up_w,
           L0_ffn_down_w, L0_ffn_gate_scale, L0_ffn_up_scale, L0_ffn_down_scale):
    import concourse.bacc as bacc
    from concourse.bass_utils import run_bass_kernel_spmd

    c = np.ascontiguousarray
    order = np.concatenate([np.arange(0, ROT, 2), np.arange(1, ROT, 2), np.arange(ROT, D)])
    order3 = np.concatenate([order, D + order, 2 * D + order])
    b_in = np.asarray(L0_attn_b_in)[order3]
    cos, sin = rotation_tables()
    arrays = {
        "x": c(np.asarray(L0_attn_X).reshape(B * S, D)),
        "w_in_t": c(np.asarray(L0_attn_W_in)[order3].T),
        "b_qc": c(b_in[0:D].reshape(KC, P).T),
        "b_k": c(b_in[D:2 * D]),
        "b_v": c(b_in[2 * D:3 * D]),
        "w_out_t": c(np.asarray(L0_attn_W_out).T[order]),
        "b_out": c(np.asarray(L0_attn_b_out)),
        "gate_w": c(np.asarray(L0_ffn_gate_w)),
        "up_w": c(np.asarray(L0_ffn_up_w)),
        "down_w": c(np.asarray(L0_ffn_down_w)),
        "gate_s": c(np.asarray(L0_ffn_gate_scale).reshape(IB, P).T),
        "up_s": c(np.asarray(L0_ffn_up_scale).reshape(IB, P).T),
        "down_s": c(np.asarray(L0_ffn_down_scale)),
        "cos_f": c(cos.T),
        "sin_f": c(sin.T),
        "cos_t": c(cos.reshape(TPB, P, HALF).transpose(1, 0, 2)),
        "sin_t": c(sin.reshape(TPB, P, HALF).transpose(1, 0, 2)),
    }
    nc = bacc.Bacc("TRN2", target_bir_lowering=False, num_devices=1)
    args = [nc.dram_tensor(n, a.shape, mybir.dt.from_np(a.dtype), kind="ExternalInput").ap() for n, a in arrays.items()]
    args.append(nc.dram_tensor("out", (B * S, D), F32, kind="ExternalOutput").ap())
    build(nc, *args)
    r = run_bass_kernel_spmd(nc, [arrays], core_ids=[0])
    return r.results[0]["out"].reshape(B, S, D)
```

```python
from contextlib import ExitStack

import numpy as np

import concourse.bass as bass
from concourse import mybir

P = 128
B, S, D, I = 2, 1024, 512, 1536
KC = D // P
IB = I // P
CH = 512
NCH = B * S // CH
TPC = CH // P
NT = B * S // P
TPB = S // P
ROT = D // 2
HALF = ROT // 2
IPP = KC
NPI = IB // IPP

F32 = mybir.dt.float32
F16 = mybir.dt.float16
BF16 = mybir.dt.bfloat16
U16 = mybir.dt.uint16
U32 = mybir.dt.uint32
ALU = mybir.AluOpType
ACT = mybir.ActivationFunctionType
AX_X = mybir.AxisListType.X
RMAX = bass.bass_isa.ReduceOp.max
RADD = bass.bass_isa.ReduceOp.add

LN_EPS = 1e-5
EXPONENT = 0x7F800000
EXPONENT_16 = 0x7F80
HALF_BIT_16 = 0x0040
MAGIC_UP = float(2 ** 20)
MAGIC_MIN = 1.5 * 2.0 ** 14
TINY = 2.0 ** -60
F16_MAX = 65504.0

PIECES = ([("k", 0), ("v", 0)] + [(w, n) for n in range(NPI) for w in "gu"]
          + [("d", 0), ("q", 0), ("d", 1), ("d", 2), ("o", 0)])
PIECE = {key: n for n, key in enumerate(PIECES)}
QUANT = [key for key in PIECES if key[0] in "gud"]
NK = 3
NMAGIC = 6
NRAW = 3

ROUND_KV = [0, 2, 0, 2, 2, 2, 2, 2]
ROUND_GU = [2, 2, 2, 2, 2, 2, 2, 0, 2, 0, 0, 0]
ROUND_Q = [2, 2, 2, 2]
SCALE_LEAD = 2


def round_range(step):
    counts = ROUND_KV + ROUND_GU + ROUND_Q
    n = sum(counts[:step])
    return n, n + counts[step]


RING_A = ([("gate", 0, i) for i in range(IB)] + [("q", 0, m) for m in range(KC)] + [("asum", 0, 0)]
          + [("gate", 1, i) for i in range(IB)] + [("q", 1, m) for m in range(KC)])
KV_TILES = [[(w, c, t) for t in range(TPC) for w in "kv"] for c in range(2)]
UP_BLOCKS = [("up", 0, i) for i in range(IB)]
RING_B_REST = ([("down", 0, t) for t in range(TPC)] + [("out", 0, t) for t in range(TPC)]
               + [("up", 1, i) for i in range(IB)]
               + [("down", 1, t) for t in range(TPC)] + [("out", 1, t) for t in range(TPC)])
RING_B = [KV_TILES[0] + KV_TILES[1] + UP_BLOCKS + RING_B_REST,
          KV_TILES[0] + UP_BLOCKS + KV_TILES[1] + RING_B_REST]
PLACE_A = {key: n for n, key in enumerate(RING_A)}
PLACE_B = [{key: n for n, key in enumerate(ring)} for ring in RING_B]
NA, NB = 2, 4


def at_a(kind, j, n):
    return (j // 2) * len(RING_A) + PLACE_A[(kind, j % 2, n)]


def at_b(kind, j, n):
    return (j // 2) * len(RING_B[0]) + PLACE_B[j // 2][(kind, j % 2, n)]


def quant_at(key, k):
    return QUANT.index(key) * KC + k


def build(nc, x, w_in_t, b_qc, b_k, b_v, w_out_t, b_out, gate_w, up_w, down_w, gate_s, up_s, down_s,
          cos_f, sin_f, cos_t, sin_t, out):
    with ExitStack() as ctx:
        def sb(name, shape, dt=F32):
            return ctx.enter_context(nc.sbuf_tensor(name, shape, dt))

        def psum(name, shape, dt=F32):
            return ctx.enter_context(nc.psum_tensor(name, shape, dt))

        def sem(name):
            return ctx.enter_context(nc.semaphore(name))

        wg = sb("wg", [P, KC, I], F16)
        wu = sb("wu", [P, KC, I], F16)
        wd = sb("wd", [P, IB, D], BF16)
        wi_hi = sb("wi_hi", [P, KC, 3 * D], F16)
        wi_lo = sb("wi_lo", [P, KC, 3 * D], F16)
        wo_hi = sb("wo_hi", [P, KC, D], F16)
        wo_lo = sb("wo_lo", [P, KC, D], F16)
        raw = sb("raw", [P, NRAW, KC, D])
        xb = raw[:, 0, :, :]
        xf = raw[:, 1, :, :]
        gg = raw[:, 2, :, :]
        xt_hi = sb("xt_hi", [P, 2, KC, CH], F16)
        xt_lo = sb("xt_lo", [P, 2, KC, CH], F16)
        x_in = sb("x_in", [P, TPC, D])
        q32 = x_in
        xn_hl = sb("xn_hl", [P, 2, 2, D], F16)
        bn6 = sb("bn6", [P, 2, 6])
        mv = sb("mv", [P, NT, 2])
        veps = sb("veps", [P, NT])
        rstd = sb("rstd", [P, NT])
        shift = sb("shift", [P, NT])
        cosf = sb("cosf", [P, S])
        sinf = sb("sinf", [P, S])
        cost = sb("cost", [P, TPB, HALF])
        sint = sb("sint", [P, TPB, HALF])
        bk_row = sb("bk_row", [P, D])
        bv_row = sb("bv_row", [P, D])
        bo_row = sb("bo_row", [P, D])
        ds_row = sb("ds_row", [P, D])
        kv_or_y = sb("kv_or_y", [P, NK + 2, D])
        kk = kv_or_y[:, 0:NK, :]
        vv = kv_or_y[:, NK, :]
        square = kv_or_y[:, NK + 1, :]
        y_halves = kv_or_y[:, 0:4, :].rearrange("p a e -> p (a e)").bitcast(F16)
        y_hi = y_halves[:, 0:KC * CH].rearrange("p (m t) -> p m t", m=KC)
        y_lo = y_halves[:, KC * CH:2 * KC * CH].rearrange("p (m t) -> p m t", m=KC)
        kcos = sb("kcos", [P, 2, HALF])
        ksin = sb("ksin", [P, 2, HALF])
        ksq = sb("ksq", [P, NT])
        krn = sb("krn", [P, NT])
        kv_sum = sb("kv_sum", [P, D])
        fu_hi = sb("fu_hi", [P, IB, CH], F16)
        fu_lo = sb("fu_lo", [P, IB, CH], F16)
        gate_work = sb("gate_work", [P, 4, CH])
        silu_g = gate_work[:, 0:2, :]
        fuse = gate_work[:, 2:4, :]
        qtmp = gate_work[:, 0:3, :]
        yy = sb("yy", [P, 3, D])
        magic = yy.rearrange("p a e -> p (a e)").bitcast(BF16).rearrange("p (a e) -> p a e", e=D)
        msum = sb("msum", [P, 2, D])
        ident = sb("ident", [P, P], F16)
        ones = sb("ones", [P, 1])
        mhalf = sb("mhalf", [P, 2])
        gs = sb("gs", [P, IB])
        ngs = sb("ngs", [P, IB])
        us = sb("us", [P, IB])
        nus = sb("nus", [P, IB])
        bq = sb("bq", [P, KC])
        ssq = sb("ssq", [P, 13, KC])
        ssqp = sb("ssqp", [P, 13])
        norm2 = sb("norm2", [P, 13])
        rnorm = sb("rnorm", [P, 13])
        mx = sb("mx", [P, 8])
        mr = sb("mr", [P, 8])
        room = sb("room", [P, 2])
        qmax = sb("qmax", [P, 2])
        inv = sb("inv", [P, 16])
        scl = sb("scl", [P, 16])
        asum = sb("asum", [P, 2, KC])
        asc = sb("asc", [P, 2, KC])

        ring_a = [psum(f"ring_a{n}", [P, 512]) for n in range(NA)]
        banks_b = psum("banks_b", [P, NB, 512])
        ring_b = [banks_b[:, n, :] for n in range(NB)]
        turn = [psum(f"turn{n}", [P, 2, KC, P], F16) for n in range(2)]

        x_landed = [sem(f"x_landed{n}") for n in range(4)]
        xf_landed = [sem(f"xf_landed{n}") for n in range(TPC)]
        raw_landed = [sem(f"raw_landed{n}") for n in range(NRAW)]
        small_landed = sem("small_landed")
        table_t_landed = sem("table_t_landed")
        table_f_landed = sem("table_f_landed")
        out_stored = [sem(f"out_stored{n}") for n in range(3)]
        ident_zero = sem("ident_zero")
        ident_ready = sem("ident_ready")
        consts_ready = sem("consts_ready")
        stats_ready = sem("stats_ready")
        rstd_ready = sem("rstd_ready")
        xn_ready = sem("xn_ready")
        xn_hi_ready = sem("xn_hi_ready")
        xn_lo_ready = sem("xn_lo_ready")
        turned = sem("turned")
        xt_ready = sem("xt_ready")
        a_full = sem("a_full")
        b_full = sem("b_full")
        v_ready = sem("v_ready")
        scaled_up = sem("scaled_up")
        rounded = sem("rounded")
        w_hi_ready = sem("w_hi_ready")
        w_lo_ready = sem("w_lo_ready")
        wd_ready = sem("wd_ready")
        squares_ready = sem("squares_ready")
        ssqp_ready = sem("ssqp_ready")
        rnorm_ready = sem("rnorm_ready")
        part_max = sem("part_max")
        all_max = sem("all_max")
        x_shifted = sem("x_shifted")
        scale_ready = sem("scale_ready")
        k_rotated = sem("k_rotated")
        k_ready = sem("k_ready")
        ksq_ready = sem("ksq_ready")
        krn_ready = sem("krn_ready")
        kv_ready = sem("kv_ready")
        kv_added = sem("kv_added")
        asum_ready = sem("asum_ready")
        asc_ready = sem("asc_ready")
        silu_ready = sem("silu_ready")
        fuse_ready = sem("fuse_ready")
        fu_hi_ready = sem("fu_hi_ready")
        fu_lo_ready = sem("fu_lo_ready")
        q_ready = sem("q_ready")
        q_rotated = sem("q_rotated")
        y_hi_ready = sem("y_hi_ready")
        y_lo_ready = sem("y_lo_ready")
        down_ready = sem("down_ready")
        g_ready = sem("g_ready")
        xb_ready = sem("xb_ready")
        y_ready = sem("y_ready")
        yg_ready = sem("yg_ready")
        out_ready = sem("out_ready")
        dve_done = sem("dve_done")
        pool_done = sem("pool_done")

        NORMS = [("k", [("k", 0)]), ("v", [("v", 0)])] + [(f"f{n}", [("g", n), ("u", n)]) for n in range(NPI)] \
            + [("q", [("q", 0)]), ("o", [("o", 0)])]
        ORD = {name: n for n, (name, _) in enumerate(NORMS)}
        MAXIMA = [("scales", 0, 3), ("a0", 3, 1), ("a1", 4, 1)]
        COL = {name: first for name, first, _ in MAXIMA}
        MORD = {name: n for n, (name, _, _) in enumerate(MAXIMA)}
        SC = {"k": 0, "v": 1, "f0": 2, "f1": 3, "f2": 4, "q": 5, "o": 6, "y0": 7, "y1": 8}

        LOW_BY_VECTOR = range(2 * TPC)
        NORMS_AT = {2: "f1", 6: "f2", 7: "q"}
        SUMMED = [key for _, pieces in NORMS for key in pieces]

        SPLIT_SQUARES = [("k", 0), ("v", 0)]
        BY_SCALAR = [(key, k) for key in SUMMED for k in range(KC) if k < 2 or key not in SPLIT_SQUARES]

        def scalar_squares(key):
            return sum(SUMMED.index(piece) <= SUMMED.index(key) for piece, _ in BY_SCALAR)

        def squares_place(key):
            kind, n = key
            if kind in "gu":
                return (wg if kind == "g" else wu)[:, :, n * D:(n + 1) * D]
            return split_of(key)[0]

        def raw_of(key):
            return raw[:, PIECE[key] % NRAW, :, :]

        def wait_raw(eng, key):
            eng.wait_ge(raw_landed[PIECE[key] % NRAW], 16 * (PIECE[key] // NRAW + 1))

        def raw_source(key):
            kind, n = key
            if kind in "qkv":
                c = "qkv".index(kind) * D
                return w_in_t[:, c:c + D].rearrange("(k p) e -> p k e", p=P)
            if kind == "o":
                return w_out_t.rearrange("(k p) e -> p k e", p=P)
            if kind == "d":
                return down_w[n * D:(n + 1) * D, :].rearrange("(k p) e -> p k e", p=P)
            src = gate_w if kind == "g" else up_w
            return src[:, n * D:(n + 1) * D].rearrange("(k p) i -> p k i", p=P)

        def split_of(key):
            kind = key[0]
            if kind == "o":
                return wo_hi[:, :, :], wo_lo[:, :, :], 3
            c = "qkv".index(kind) * D
            return wi_hi[:, :, c:c + D], wi_lo[:, :, c:c + D], "kvq".index(kind)

        def wait_converted(eng, key):
            if key in QUANT:
                eng.wait_ge(rounded, quant_at(key, KC - 1) + 1)
            else:
                eng.wait_ge(w_lo_ready, KC * (split_of(key)[2] + 1))

        block = ctx.enter_context(nc.Block())

        @block.sync
        def _(sp):
            def load_x(t):
                if t >= TPC:
                    sp.wait_ge(xn_lo_ready, t - TPC + 1)
                if t >= 2 * TPC and t % TPC == 0:
                    sp.wait_ge(y_hi_ready, KC * (t // TPC - 1))
                    sp.wait_ge(y_lo_ready, KC * (t // TPC - 1))
                sp.dma_start(x_in[:, t % TPC, :], x[t * P:(t + 1) * P, :]).then_inc(x_landed[t % 4], 16)

            def load_piece(n):
                if n >= NRAW:
                    wait_converted(sp, PIECES[n - NRAW])
                sp.dma_start(raw[:, n % NRAW, :, :], raw_source(PIECES[n])).then_inc(raw_landed[n % NRAW], 16)

            def load_xf(t):
                if t == 0:
                    wait_converted(sp, ("d", 1))
                if t >= TPC:
                    sp.wait_ge(out_ready, t - TPC + 1)
                sp.dma_start(xf[:, t % TPC, :], x[t * P:(t + 1) * P, :]).then_inc(xf_landed[t % TPC], 16)

            def store(t):
                sp.wait_ge(out_ready, t + 1)
                sp.dma_start(out[t * P:(t + 1) * P, :], yy[:, t % 3, :]).then_inc(out_stored[t % 3], 16)

            for t in range(4):
                load_x(t)
            load_piece(0)
            load_piece(1)
            load_piece(2)
            for dst, src in ((gs, gate_s), (us, up_s), (bq, b_qc)):
                sp.dma_start(dst[:, :], src).then_inc(small_landed, 16)
            for row, src in ((bk_row, b_k), (bv_row, b_v), (ds_row, down_s), (bo_row, b_out)):
                sp.dma_start(row[:, :], src.rearrange("(a e) -> a e", a=1).broadcast_to([P, D]))\
                    .then_inc(small_landed, 16)
            for t in range(TPC, 2 * TPC):
                load_x(t)
            sp.dma_start(cost[:, :, :], cos_t).then_inc(table_t_landed, 16)
            sp.dma_start(sint[:, :, :], sin_t).then_inc(table_t_landed, 16)
            for n in range(3, 9):
                load_piece(n)
            sp.dma_start(cosf[:, :], cos_f).then_inc(table_f_landed, 16)
            sp.dma_start(sinf[:, :], sin_f).then_inc(table_f_landed, 16)
            for n in range(9, len(PIECES)):
                load_piece(n)
            for t in range(TPC):
                load_xf(t)
            for j in range(NCH):
                for t in range(j * TPC, (j + 1) * TPC):
                    if j < NCH - 2:
                        load_x(t + 2 * TPC)
                    store(t)
                    if t + TPC < NT:
                        load_xf(t + TPC)
            for n in range(3):
                sp.wait_ge(out_stored[n], 16 * len(range(n, NT, 3)))

        @block.gpsimd
        def _(pool):
            own = [0]

            def done(ins):
                own[0] += 1
                ins.then_inc(pool_done, 1)
                return own[0]

            pool.memset(ident[:, :], 0.0).then_inc(ident_zero, 1)
            pool.memset(ones[:, :], 1.0).then_inc(consts_ready, 1)
            pool.memset(mhalf[:, :], -0.5).then_inc(consts_ready, 1)
            pool.wait_ge(ident_zero, 1)
            pool.affine_select(out=ident[:, :], in_=ident[:, :], compare_op=ALU.not_equal, fill=1.0, base=0,
                               pattern=[[-1, P]], channel_multiplier=1).then_inc(ident_ready, 1)
            pool.wait_ge(consts_ready, 2)

            def rsqrt_var(t):
                pool.wait_ge(stats_ready, t + 1)
                n = done(pool.tensor_scalar(veps[:, t:t + 1], mv[:, t, 1:2], LN_EPS, 1.0, ALU.add, ALU.mult))
                pool.wait_ge(pool_done, n)
                pool.tensor_tensor(rstd[:, t:t + 1], veps[:, t:t + 1], mhalf[:, 0:1], ALU.pow).then_inc(rstd_ready, 1)

            def xn_low(t):
                pool.wait_ge(xn_hi_ready, t + 1)
                pool.tensor_tensor(xn_hl[:, t % 2, 1, :], x_in[:, t % TPC, :], xn_hl[:, t % 2, 0, :], ALU.subtract)\
                    .then_inc(xn_lo_ready, 1)

            def shift_of(t):
                pool.wait_ge(rstd_ready, t + 1)
                done(pool.tensor_scalar(shift[:, t:t + 1], mv[:, t, 0:1], rstd[:, t:t + 1], -1.0, ALU.mult, ALU.mult))

            def norm_step(j, step):
                if step < TPC:
                    rsqrt_var(j * TPC + step)
                if 1 <= step:
                    t = j * TPC + step - 1
                    if t not in LOW_BY_VECTOR:
                        xn_low(t)
                    shift_of(t)

            def norms(name):
                pieces = NORMS[ORD[name]][1]
                c, n = PIECE[pieces[0]], len(pieces)
                cols = slice(c, c + n)
                pool.wait_ge(ssqp_ready, ORD[name] + 1)
                m = done(pool.partition_all_reduce(norm2[:, cols], ssqp[:, cols], P, RADD))
                pool.wait_ge(pool_done, m)
                more = (1.25, 3.0) if n == 2 else (1.0, TINY)
                m = done(pool.tensor_scalar(norm2[:, cols], norm2[:, cols], more[0], more[1], ALU.mult, ALU.add))
                pool.wait_ge(pool_done, m)
                pool.tensor_tensor(rnorm[:, cols], norm2[:, cols], mhalf[:, 0:n], ALU.pow).then_inc(rnorm_ready, 1)

            def maximum(name):
                c, n = COL[name], MAXIMA[MORD[name]][2]
                pool.wait_ge(part_max, MORD[name] + 1)
                pool.partition_all_reduce(mr[:, c:c + n], mx[:, c:c + n], P, RMAX).then_inc(all_max, 1)

            def rotate_k(t):
                if t == 0:
                    pool.wait_ge(table_t_landed, 32)
                else:
                    pool.wait_ge(k_rotated, 2 * t)
                pool.wait_ge(k_ready, t + 1)
                k = kk[:, t % NK, 0:ROT].rearrange("p (a f) -> p a f", a=2)
                c, s = cost[:, t % TPB, :], sint[:, t % TPB, :]
                for a in range(2):
                    done(pool.tensor_tensor(kcos[:, a, :], k[:, a, :], c, ALU.mult))
                    n = done(pool.tensor_tensor(ksin[:, a, :], k[:, a, :], s, ALU.mult))
                norm_k(t)
                pool.wait_ge(pool_done, n)
                pool.tensor_tensor(k[:, 0, :], kcos[:, 0, :], ksin[:, 1, :], ALU.subtract).then_inc(k_rotated, 1)
                pool.tensor_tensor(k[:, 1, :], kcos[:, 1, :], ksin[:, 0, :], ALU.add).then_inc(k_rotated, 1)

            def norm_k(t):
                pool.wait_ge(ksq_ready, t + 1)
                n = done(pool.tensor_tensor(krn[:, t:t + 1], ksq[:, t:t + 1], mhalf[:, 0:1], ALU.pow))
                pool.wait_ge(pool_done, n)
                pool.tensor_scalar(krn[:, t:t + 1], krn[:, t:t + 1], 1e12, 0.0, ALU.min, ALU.max)\
                    .then_inc(krn_ready, 1)

            def add_kv(t):
                pool.wait_ge(kv_ready, t + 1)
                if t % TPB == 0:
                    if t:
                        pool.wait_ge(a_full, at_a("asum", 0, 0) + 1)
                    pool.tensor_copy(kv_sum[:, :], kk[:, t % NK, :]).then_inc(kv_added, 1)
                else:
                    pool.wait_ge(kv_added, t)
                    pool.tensor_tensor(kv_sum[:, :], kv_sum[:, :], kk[:, t % NK, :], ALU.add).then_inc(kv_added, 1)

            def kv(j):
                for t in range(j * TPC, (j + 1) * TPC):
                    rotate_k(t)
                    if t % TPC:
                        add_kv(t - 1)
                add_kv(t)

            def kv_first():
                rsqrt_var(TPC)
                for t in range(TPB):
                    if t < TPC - 1:
                        rsqrt_var(TPC + t + 1)
                    rotate_k(t)
                    if t:
                        add_kv(t - 1)
                    if t < TPC:
                        shift_of(TPC + t)
                    if t == 1:
                        maximum("scales")
                    if t == TPB - 2:
                        norms("f0")
                add_kv(t)

            def rotate_q(j):
                if j == 0:
                    pool.wait_ge(table_f_landed, 32)
                pool.wait_ge(fu_lo_ready, IB * (j + 1))
                pool.wait_ge(fu_hi_ready, IB * (j + 1))
                c0 = (j % 2) * CH
                c, s = cosf[:, c0:c0 + CH], sinf[:, c0:c0 + CH]
                pool.wait_ge(q_ready, KC * j + 2)
                done(pool.tensor_tensor(qtmp[:, 0, :], q32[:, 0, :], c, ALU.mult))
                done(pool.tensor_tensor(qtmp[:, 1, :], q32[:, 1, :], s, ALU.mult))
                n = done(pool.tensor_tensor(qtmp[:, 2, :], q32[:, 0, :], s, ALU.mult))
                pool.wait_ge(pool_done, n)
                pool.tensor_tensor(q32[:, 0, :], qtmp[:, 0, :], qtmp[:, 1, :], ALU.subtract).then_inc(q_rotated, 1)
                pool.wait_ge(q_rotated, 2 * j + 1)
                n = done(pool.tensor_tensor(qtmp[:, 0, :], q32[:, 1, :], c, ALU.mult))
                pool.wait_ge(pool_done, n)
                pool.tensor_tensor(q32[:, 1, :], qtmp[:, 0, :], qtmp[:, 2, :], ALU.add).then_inc(q_rotated, 1)

            def residual(t):
                if t == 0:
                    pool.wait_ge(small_landed, 16 * 7)
                pool.wait_ge(x_shifted, t + 1)
                pool.tensor_tensor(xb[:, t % TPC, :], xb[:, t % TPC, :], bo_row[:, :], ALU.add).then_inc(xb_ready, 1)

            def finish(t):
                pool.wait_ge(yg_ready, t + 1)
                pool.tensor_tensor(yy[:, t % 3, :], yy[:, t % 3, :], xf[:, t % TPC, :], ALU.add).then_inc(out_ready, 1)

            def fuse_low(j, i):
                n = IB * j + i
                pool.wait_ge(fuse_ready, n + 1)
                pool.wait_ge(fu_hi_ready, n + 1)
                pool.tensor_tensor(fu_lo[:, i, :], fuse[:, n % 2, :], fu_hi[:, i, :], ALU.subtract)\
                    .then_inc(fu_lo_ready, 1)

            for step in range(TPC + 1):
                norm_step(0, step)
            norms("k")
            norms("v")
            for j in range(NCH):
                if j == 0:
                    kv_first()
                elif j == 2:
                    kv(j)
                for i in range(IB):
                    if j == 0 and i:
                        fuse_low(j, i - 1)
                    if 1 <= j < NCH - 1 and i < TPC + 1:
                        norm_step(j + 1, i)
                    if j == 0 and i in NORMS_AT:
                        norms(NORMS_AT[i])
                if j == 0:
                    fuse_low(j, IB - 1)
                if j == 2:
                    kv(j + 1)
                rotate_q(j)
                if j == 0:
                    norms("o")
                if j % 2 == 0:
                    maximum(f"a{j // 2}")
                for t in range(j * TPC, (j + 1) * TPC):
                    residual(t)
                if j < NCH - 1:
                    for t in range(j * TPC, (j + 1) * TPC):
                        finish(t)

        @block.scalar
        def _(act):
            def xn_high(t):
                act.wait_ge(xn_ready, t + 1)
                if t >= 2:
                    act.wait_ge(turned, t - 1)
                nc.scalar.activation(xn_hl[:, t % 2, 0, :], x_in[:, t % TPC, :], ACT.Copy).then_inc(xn_hi_ready, 1)

            def evacuate_turned(t):
                act.wait_ge(turned, t + 1)
                c = (t % TPC) * P
                nc.scalar.activation(xt_hi[:, (t // TPC) % 2, :, c:c + P], turn[t % 2][:, 0, :, :], ACT.Copy)
                nc.scalar.activation(xt_lo[:, (t // TPC) % 2, :, c:c + P], turn[t % 2][:, 1, :, :], ACT.Copy)\
                    .then_inc(xt_ready, 1)

            def sum_squares(key):
                wait_raw(act, key)
                for k in range(2 if key in SPLIT_SQUARES else KC):
                    nc.scalar.activation(squares_place(key)[:, k, :], raw_of(key)[:, k, :], ACT.Square,
                                         accum_out=ssq[:, PIECE[key], k:k + 1]).then_inc(squares_ready, 1)

            def scale_up(n0, n1):
                for n in range(n0, n1):
                    key, k = QUANT[n // KC], n % KC
                    if k == 0:
                        if key[0] in "gu":
                            sum_squares(key)
                        wait_raw(act, key)
                    if n >= NMAGIC:
                        act.wait_ge(rounded, n - NMAGIC + 1)
                    nc.scalar.activation(magic[:, n % NMAGIC, :], raw_of(key)[:, k, :], ACT.Copy, scale=MAGIC_UP)\
                        .then_inc(scaled_up, 1)

            def weight_high(key, k0=0, k1=KC):
                hi, _, _ = split_of(key)
                act.wait_ge(scale_ready, ORD[key[0]] + 1)
                act.wait_ge(squares_ready, scalar_squares(key))
                for k in range(k0, k1):
                    nc.scalar.activation(hi[:, k, :], raw_of(key)[:, k, :], ACT.Copy,
                                         scale=scl[:, SC[key[0]]:SC[key[0]] + 1]).then_inc(w_hi_ready, 1)

            def scale_down(n):
                act.wait_ge(rounded, KC * (QUANT.index(("d", n)) + 1))
                nc.scalar.activation(wd[:, n * KC:(n + 1) * KC, :], wd[:, n * KC:(n + 1) * KC, :], ACT.Copy,
                                     scale=inv[:, SC[f"f{n}"]:SC[f"f{n}"] + 1]).then_inc(wd_ready, 1)

            def square_k(t):
                act.wait_ge(k_ready, t + 1)
                if t:
                    act.wait_ge(ksq_ready, t)
                nc.scalar.activation(square[:, :], kk[:, t % NK, :], ACT.Square, accum_out=ksq[:, t:t + 1])\
                    .then_inc(ksq_ready, 1)

            def silu_gate(j, i):
                n = IB * j + i
                act.wait_ge(a_full, at_a("gate", j, i) + 1)
                if n >= 2:
                    act.wait_ge(fuse_ready, n - 1)
                nc.scalar.activation(silu_g[:, n % 2, :], ring_a[at_a("gate", j, i) % NA][:, :], ACT.Silu,
                                     scale=ngs[:, i:i + 1]).then_inc(silu_ready, 1)

            def fuse_high(j, i):
                n = IB * j + i
                act.wait_ge(fuse_ready, n + 1)
                nc.scalar.activation(fu_hi[:, i, :], fuse[:, n % 2, :], ACT.Copy).then_inc(fu_hi_ready, 1)

            def gate_up(j):
                for i in range(IB):
                    silu_gate(j, i)
                    if i:
                        fuse_high(j, i - 1)
                    if j == 0:
                        scale_up(*round_range(TPB + i + SCALE_LEAD))
                        if i == 6:
                            sum_squares(("q", 0))
                        if i in (8, 9):
                            weight_high(("q", 0), 2 * (i - 8), 2 * (i - 7))
                    elif j + 1 < NCH:
                        if 2 <= i < 2 + TPC:
                            xn_high((j + 1) * TPC + i - 2)
                        if 6 <= i < 6 + TPC:
                            evacuate_turned((j + 1) * TPC + i - 6)
                fuse_high(j, IB - 1)

            def shift_x(t):
                act.wait_ge(xf_landed[t % TPC], 16 * (t // TPC + 1))
                if t == 0:
                    wait_converted(act, ("o", 0))
                if t >= TPC:
                    act.wait_ge(y_ready, t - TPC + 1)
                nc.scalar.activation(xb[:, t % TPC, :], xf[:, t % TPC, :], ACT.Identity, bias=shift[:, t:t + 1],
                                     scale=rstd[:, t:t + 1]).then_inc(x_shifted, 1)

            def take_q(j):
                act.wait_ge(xn_lo_ready, min(TPC * (j + 2), NT))
                for m in range(KC):
                    a = at_a("q", j, m)
                    act.wait_ge(a_full, a + 1)
                    nc.scalar.activation(q32[:, m, :], ring_a[a % NA][:, :], ACT.Identity, bias=bq[:, m:m + 1],
                                         scale=inv[:, SC["q"]:SC["q"] + 1]).then_inc(q_ready, 1)
                    if j == 0:
                        if m < KC - SCALE_LEAD:
                            scale_up(*round_range(TPB + IB + m + SCALE_LEAD))
                        if m % 2:
                            scale_down(m // 2)

            def y_high(j):
                act.wait_ge(asc_ready, j // 2 + 1)
                for m in (2, 3, 0, 1):
                    if m < 2:
                        act.wait_ge(q_rotated, 2 * j + m + 1)
                    else:
                        act.wait_ge(q_ready, KC * j + m + 1)
                    nc.scalar.activation(y_hi[:, m, :], q32[:, m, :], ACT.Copy, scale=asc[:, j // 2, m:m + 1])\
                        .then_inc(y_hi_ready, 1)

            def silu_down(j):
                for t in range(j * TPC, (j + 1) * TPC):
                    act.wait_ge(down_ready, t + 1)
                    nc.scalar.activation(gg[:, t % TPC, :], gg[:, t % TPC, :], ACT.Silu, scale=-1.0)\
                        .then_inc(g_ready, 1)

            xn_high(0)
            xn_high(1)
            sum_squares(("k", 0))
            evacuate_turned(0)
            xn_high(2)
            evacuate_turned(1)
            xn_high(3)
            sum_squares(("v", 0))
            weight_high(("k", 0))
            evacuate_turned(2)
            evacuate_turned(3)
            weight_high(("v", 0))
            for step in range(SCALE_LEAD):
                scale_up(*round_range(step))
            for j in range(NCH):
                if j == 0:
                    for t in range(TPB):
                        square_k(t)
                        if t < TPC:
                            xn_high(TPC + t)
                        if TPC <= t + 2 < 2 * TPC:
                            evacuate_turned(t + 2)
                        scale_up(*round_range(t + SCALE_LEAD))
                elif j == 2:
                    for t in range(j * TPC, (j + 1) * TPC):
                        square_k(t)
                gate_up(j)
                if j == 2:
                    for t in range((j + 1) * TPC, (j + 2) * TPC):
                        square_k(t)
                take_q(j)
                if j == 0:
                    sum_squares(("o", 0))
                    scale_down(2)
                    weight_high(("o", 0))
                if j % 2 == 0:
                    a = at_a("asum", j, 0)
                    act.wait_ge(a_full, a + 1)
                    nc.scalar.activation(asum[:, j // 2, :], ring_a[a % NA][:, 0:KC], ACT.Copy)\
                        .then_inc(asum_ready, 1)
                y_high(j)
                for t in range(j * TPC, (j + 1) * TPC):
                    shift_x(t)
                silu_down(j)

        @block.vector
        def _(dve):
            own = [0]

            def done(ins):
                own[0] += 1
                ins.then_inc(dve_done, 1)
                return own[0]

            def then(ins):
                dve.wait_ge(dve_done, done(ins))

            def statistics(t):
                dve.wait_ge(x_landed[t % 4], 16 * (t // 4 + 1))
                then(dve.bn_stats(bn6[:, t % 2, :], x_in[:, t % TPC, :]))
                dve.bn_aggr(mv[:, t, :], bn6[:, t % 2, :]).then_inc(stats_ready, 1)

            def normalise(t):
                dve.wait_ge(rstd_ready, t + 1)
                dve.wait_ge(stats_ready, t + 1)
                dve.tensor_scalar(x_in[:, t % TPC, :], x_in[:, t % TPC, :], mv[:, t, 0:1], rstd[:, t:t + 1],
                                  ALU.subtract, ALU.mult).then_inc(xn_ready, 1)

            def xn_low(t):
                dve.wait_ge(xn_hi_ready, t + 1)
                dve.wait_ge(xn_ready, t + 1)
                dve.tensor_tensor(xn_hl[:, t % 2, 1, :], x_in[:, t % TPC, :], xn_hl[:, t % 2, 0, :], ALU.subtract)\
                    .then_inc(xn_lo_ready, 1)

            def norm_step(j, step):
                if step < TPC:
                    statistics(j * TPC + step)
                if 1 <= step < TPC + 1:
                    normalise(j * TPC + step - 1)
                t = j * TPC + step - 2
                if step >= 2 and t in LOW_BY_VECTOR:
                    xn_low(t)

            def sum_squares(key):
                wait_raw(dve, key)
                for k in range(2, KC):
                    w = raw_of(key)[:, k, :]
                    n = done(dve.scalar_tensor_tensor(squares_place(key)[:, k, :], w, 1.0, w, ALU.mult, ALU.mult,
                                                      accum_out=ssq[:, PIECE[key], k:k + 1]))
                dve.wait_ge(dve_done, n)

            def add_squares(name):
                pieces = NORMS[ORD[name]][1]
                c, n = PIECE[pieces[0]], len(pieces)
                dve.wait_ge(squares_ready, scalar_squares(pieces[-1]))
                dve.tensor_reduce(ssqp[:, c:c + n], ssq[:, c:c + n, :], AX_X, ALU.add).then_inc(ssqp_ready, 1)

            def power_of(ap):
                then(dve.tensor_scalar(ap.bitcast(U32), ap.bitcast(U32), EXPONENT, None, ALU.bitwise_and))

            def piece_scale(kind):
                c, r = SC[kind], rnorm[:, PIECE[(kind, 0)]:PIECE[(kind, 0)] + 1]
                dve.wait_ge(rnorm_ready, ORD[kind] + 1)
                power_of(r)
                then(dve.tensor_scalar(scl[:, c:c + 1], r, 2.0 ** 15, None, ALU.mult))
                dve.reciprocal(inv[:, c:c + 1], scl[:, c:c + 1]).then_inc(scale_ready, 1)

            def weight_low(key, k0=0, k1=KC):
                _, lo, n = split_of(key)
                hi, _, _ = split_of(key)
                dve.wait_ge(scale_ready, ORD[key[0]] + 1)
                for k in range(k0, k1):
                    dve.wait_ge(w_hi_ready, KC * n + k + 1)
                    dve.scalar_tensor_tensor(lo[:, k, :], raw_of(key)[:, k, :], scl[:, SC[key[0]]:SC[key[0]] + 1],
                                             hi[:, k, :], ALU.mult, ALU.subtract).then_inc(w_lo_ready, 1)

            def small_maxima():
                for c, src in enumerate((gs, us, bq)):
                    ins = dve.tensor_reduce(mx[:, c:c + 1], src[:, :], AX_X, ALU.max, apply_absolute_value=True)
                    if c < 2:
                        done(ins)
                dve.wait_ge(dve_done, own[0])
                ins.then_inc(part_max, 1)

            def ffn_room():
                dve.wait_ge(all_max, MORD["scales"] + 1)
                then(dve.tensor_tensor(room[:, 0:1], mr[:, 0:1], mr[:, 1:2], ALU.mult))
                then(dve.tensor_scalar(room[:, 0:1], room[:, 0:1], TINY, D / (F16_MAX * 0.99), ALU.max, ALU.mult))
                then(dve.reciprocal(room[:, 1:2], room[:, 0:1]))

            def ffn_scale(n):
                c, r = SC[f"f{n}"], PIECE[("g", n)]
                dve.wait_ge(rnorm_ready, ORD[f"f{n}"] + 1)
                then(dve.scalar_tensor_tensor(scl[:, c:c + 1], rnorm[:, r:r + 1], room[:, 1:2], rnorm[:, r + 1:r + 2],
                                              ALU.mult, ALU.mult))
                power_of(scl[:, c:c + 1])
                then(dve.reciprocal(inv[:, c:c + 1], scl[:, c:c + 1]))
                dve.tensor_scalar(nus[:, n * IPP:(n + 1) * IPP], us[:, n * IPP:(n + 1) * IPP],
                                  scl[:, c:c + 1], -1.0, ALU.mult, ALU.mult).then_inc(scale_ready, 1)

            def quantised(key, k):
                kind, n = key
                if kind == "d":
                    return wd[:, n * KC + k, :]
                return (wg if kind == "g" else wu)[:, k, n * D:(n + 1) * D]

            def quantise(n0, n1):
                for pair in range(n0, n1, 2):
                    blocks = range(pair, min(pair + 2, n1))
                    made, summed = {}, {}
                    for n in blocks:
                        m = magic[:, n % NMAGIC, :].bitcast(U16)
                        dve.wait_ge(scaled_up, n + 1)
                        made[n] = done(dve.tensor_scalar(m, m, EXPONENT_16, HALF_BIT_16, ALU.bitwise_and,
                                                         ALU.bitwise_or))
                    for n in blocks:
                        key = QUANT[n // KC]
                        wait_raw(dve, key)
                        dve.wait_ge(dve_done, made[n])
                        if n >= 2:
                            dve.wait_ge(rounded, n - 1)
                        summed[n] = done(dve.scalar_tensor_tensor(
                            msum[:, n % 2, :], magic[:, n % NMAGIC, :], MAGIC_MIN, raw_of(key)[:, n % KC, :],
                            ALU.max, ALU.add))
                    for n in blocks:
                        key = QUANT[n // KC]
                        if key[0] in "gu":
                            dve.wait_ge(squares_ready, scalar_squares(key))
                        dve.wait_ge(dve_done, summed[n])
                        dve.scalar_tensor_tensor(quantised(key, n % KC), magic[:, n % NMAGIC, :], MAGIC_MIN,
                                                 msum[:, n % 2, :], ALU.max, ALU.subtract).then_inc(rounded, 1)

            def take_k(t):
                j = t // TPC
                n = at_b("k", j, t % TPC)
                dve.wait_ge(b_full, n + 1)
                if t >= NK:
                    dve.wait_ge(kv_added, t - NK + 1)
                dve.scalar_tensor_tensor(kk[:, t % NK, :], ring_b[n % NB][:, :], inv[:, SC["k"]:SC["k"] + 1],
                                         bk_row[:, :], ALU.mult, ALU.add).then_inc(k_ready, 1)

            def take_v(t):
                j = t // TPC
                n = at_b("v", j, t % TPC)
                dve.wait_ge(b_full, n + 1)
                if t:
                    dve.wait_ge(kv_ready, t)
                dve.scalar_tensor_tensor(vv[:, :], ring_b[n % NB][:, :], inv[:, SC["v"]:SC["v"] + 1],
                                         bv_row[:, :], ALU.mult, ALU.add).then_inc(v_ready, 1)

            def times_v(t):
                dve.wait_ge(krn_ready, t + 1)
                dve.wait_ge(k_rotated, 2 * (t + 1))
                dve.wait_ge(v_ready, t + 1)
                dve.scalar_tensor_tensor(kk[:, t % NK, :], kk[:, t % NK, :], krn[:, t:t + 1], vv[:, :],
                                         ALU.mult, ALU.mult).then_inc(kv_ready, 1)

            def kv(j):
                for t in range(j * TPC, (j + 1) * TPC):
                    take_k(t)
                    if t % TPC:
                        times_v(t - 1)
                    take_v(t)
                times_v(t)

            def kv_first():
                for t in range(TPB):
                    if t < TPC - 1:
                        statistics(TPC + t + 1)
                    take_k(t)
                    if t < TPC:
                        normalise(TPC + t)
                    if 1 <= t < TPC + 1:
                        xn_low(TPC + t - 1)
                    quantise(*round_range(t))
                    if t == TPB - 3:
                        add_squares("f0")
                    if t:
                        times_v(t - 1)
                    take_v(t)
                times_v(t)

            def fuse_block(j, i):
                n = IB * j + i
                b = at_b("up", j, i)
                dve.wait_ge(b_full, b + 1)
                dve.wait_ge(silu_ready, n + 1)
                if n >= 2:
                    dve.wait_ge(fu_lo_ready, n - 1)
                if j == 0 and i % IPP == 0:
                    dve.wait_ge(scale_ready, ORD[f"f{i // IPP}"] + 1)
                dve.scalar_tensor_tensor(fuse[:, n % 2, :], ring_b[b % NB][:, :], nus[:, i:i + 1],
                                         silu_g[:, n % 2, :], ALU.mult, ALU.mult).then_inc(fuse_ready, 1)

            def fuse_low(j, i):
                n = IB * j + i
                dve.wait_ge(fu_hi_ready, n + 1)
                dve.tensor_tensor(fu_lo[:, i, :], fuse[:, n % 2, :], fu_hi[:, i, :], ALU.subtract)\
                    .then_inc(fu_lo_ready, 1)

            def gate_up(j):
                for i in range(IB):
                    if j and i:
                        fuse_low(j, i - 1)
                    fuse_block(j, i)
                    if j == 0:
                        if i == 8:
                            piece_scale("q")
                            q_bound()
                        quantise(*round_range(TPB + i))
                        if i + 1 in NORMS_AT:
                            add_squares(NORMS_AT[i + 1])
                        if i == 3:
                            ffn_scale(1)
                        if i == 7:
                            ffn_scale(2)
                        if i in (9, 10):
                            weight_low(("q", 0), 2 * (i - 9), 2 * (i - 8))
                    elif j + 1 < NCH and i < TPC + 1:
                        norm_step(j + 1, i)
                if j:
                    fuse_low(j, IB - 1)

            def take_down(j):
                for t in range(TPC):
                    b = at_b("down", j, t)
                    dve.wait_ge(b_full, b + 1)
                    if j:
                        dve.wait_ge(out_ready, j * TPC - TPC + t + 1)
                    dve.tensor_tensor(gg[:, t, :], ring_b[b % NB][:, :], ds_row[:, :], ALU.mult)\
                        .then_inc(down_ready, 1)

            def scale_a(b):
                c, y = COL[f"a{b}"], SC[f"y{b}"]
                dve.wait_ge(asum_ready, b + 1)
                dve.tensor_reduce(mx[:, c:c + 1], asum[:, b, :], AX_X, ALU.max, apply_absolute_value=True)\
                    .then_inc(part_max, 1)
                dve.wait_ge(all_max, MORD[f"a{b}"] + 1)
                then(dve.tensor_scalar(mr[:, c:c + 1], mr[:, c:c + 1], TINY, qmax[:, 1:2], ALU.max, ALU.mult))
                then(dve.reciprocal(scl[:, y:y + 1], mr[:, c:c + 1]))
                power_of(scl[:, y:y + 1])
                dve.tensor_scalar(asc[:, b, :], asum[:, b, :], scl[:, y:y + 1], None, ALU.mult)\
                    .then_inc(asc_ready, 1)
                then(dve.reciprocal(inv[:, y:y + 1], scl[:, y:y + 1]))
                then(dve.tensor_tensor(inv[:, y:y + 1], inv[:, y:y + 1], inv[:, SC["o"]:SC["o"] + 1], ALU.mult))

            def q_bound():
                c = SC["q"]
                dve.wait_ge(scale_ready, ORD["q"] + 1)
                then(dve.tensor_scalar(qmax[:, 0:1], inv[:, c:c + 1], 32.0, TINY, ALU.mult, ALU.add))
                then(dve.scalar_tensor_tensor(qmax[:, 1:2], mr[:, 2:3], 2.0 ** -14, qmax[:, 0:1],
                                              ALU.mult, ALU.add))

            def y_low(j):
                for n, m in enumerate((2, 3, 0, 1)):
                    dve.wait_ge(y_hi_ready, KC * j + n + 1)
                    dve.scalar_tensor_tensor(y_lo[:, m, :], q32[:, m, :], asc[:, j // 2, m:m + 1], y_hi[:, m, :],
                                             ALU.mult, ALU.subtract).then_inc(y_lo_ready, 1)

            def take_out(j):
                y = SC[f"y{j // 2}"]
                for t in range(j * TPC, (j + 1) * TPC):
                    b = at_b("out", j, t % TPC)
                    dve.wait_ge(b_full, b + 1)
                    dve.wait_ge(xb_ready, t + 1)
                    if t >= 3:
                        dve.wait_ge(out_stored[t % 3], 16 * (t // 3))
                    dve.scalar_tensor_tensor(yy[:, t % 3, :], ring_b[b % NB][:, :], inv[:, y:y + 1],
                                             xb[:, t % TPC, :], ALU.mult, ALU.add).then_inc(y_ready, 1)
                    dve.wait_ge(y_ready, t + 1)
                    dve.wait_ge(g_ready, t + 1)
                    dve.tensor_tensor(yy[:, t % 3, :], yy[:, t % 3, :], gg[:, t % TPC, :], ALU.mult)\
                        .then_inc(yg_ready, 1)
                    if j == NCH - 1:
                        dve.wait_ge(yg_ready, t + 1)
                        dve.tensor_tensor(yy[:, t % 3, :], yy[:, t % 3, :], xf[:, t % TPC, :], ALU.add)\
                            .then_inc(out_ready, 1)

            for step in range(TPC):
                norm_step(0, step)
            normalise(TPC - 1)
            sum_squares(("k", 0))
            add_squares("k")
            xn_low(TPC - 2)
            sum_squares(("v", 0))
            piece_scale("k")
            xn_low(TPC - 1)
            add_squares("v")
            weight_low(("k", 0))
            piece_scale("v")
            weight_low(("v", 0))
            dve.wait_ge(small_landed, 16 * 7)
            small_maxima()
            then(dve.tensor_scalar(ngs[:, :], gs[:, :], -1.0, None, ALU.mult))
            statistics(TPC)
            for j in range(NCH):
                if j == 0:
                    kv_first()
                    ffn_room()
                    ffn_scale(0)
                elif j == 2:
                    kv(j)
                gate_up(j)
                if j == 2:
                    kv(j + 1)
                if j == 0:
                    for m in range(KC):
                        quantise(*round_range(TPB + IB + m))
                    add_squares("o")
                    piece_scale("o")
                    weight_low(("o", 0))
                if j % 2 == 0:
                    scale_a(j // 2)
                y_low(j)
                take_down(j)
                take_out(j)

        @block.tensor
        def _(pe):
            def fill_a(kind, j, n):
                a = at_a(kind, j, n)
                if a >= NA:
                    wait_a_free(a - NA)
                return ring_a[a % NA]

            def wait_a_free(a):
                b, n = divmod(a, len(RING_A))
                kind, jj, i = RING_A[n]
                j = 2 * b + jj
                if kind == "gate":
                    pe.wait_ge(silu_ready, IB * j + i + 1)
                elif kind == "q":
                    pe.wait_ge(q_ready, KC * j + i + 1)
                else:
                    pe.wait_ge(asum_ready, b + 1)

            def wait_b_free(b):
                batch, n = divmod(b, len(RING_B[0]))
                kind, jj, i = RING_B[batch][n]
                j = 2 * batch + jj
                if kind == "up":
                    pe.wait_ge(fuse_ready, IB * j + i + 1)
                else:
                    reader = {"k": k_ready, "v": v_ready, "down": down_ready, "out": y_ready}[kind]
                    pe.wait_ge(reader, TPC * j + i + 1)

            def fill_b(kind, j, n):
                b = at_b(kind, j, n)
                if b >= NB:
                    wait_b_free(b - NB)
                return ring_b[b % NB]

            def transposes(t):
                if t == 0:
                    pe.wait_ge(ident_ready, 1)
                pe.wait_ge(xn_lo_ready, t + 1)
                pe.wait_ge(xn_hi_ready, t + 1)
                if t >= 2:
                    pe.wait_ge(xt_ready, t - 1)
                for h in range(2):
                    for k in range(KC):
                        last = pe.transpose(turn[t % 2][:, h, k, :], xn_hl[:, t % 2, h, k * P:(k + 1) * P],
                                            ident[:, :])
                last.then_inc(turned, 1)

            def products(dst, terms, start=True, stop=True):
                for n, (lhs, rhs) in enumerate(terms):
                    last = pe.matmul(dst, lhs, rhs, start=start and n == 0, stop=stop and n == len(terms) - 1)
                return last

            def kv_tile(t):
                j, c = t // TPC, (t % TPC) * P
                pe.wait_ge(xt_ready, t + 1)
                for n, w in enumerate("kv"):
                    dst = fill_b(w, j, t % TPC)
                    e = (1 + n) * D
                    terms = []
                    for k in range(KC):
                        hi, lo = xt_hi[:, j % 2, k, c:c + P], xt_lo[:, j % 2, k, c:c + P]
                        terms += [(hi, wi_hi[:, k, e:e + D]), (hi, wi_lo[:, k, e:e + D]), (lo, wi_hi[:, k, e:e + D])]
                    if t:
                        last = products(dst[:, :], terms)
                    else:
                        for k in range(KC):
                            pe.wait_ge(w_lo_ready, KC * n + k + 1)
                            last = products(dst[:, :], terms[3 * k:3 * k + 3], k == 0, k == KC - 1)
                    last.then_inc(b_full, 1)

            def gate_up(j):
                pe.wait_ge(xt_ready, TPC * (j + 1))
                for i in range(IB):
                    for kind, w, fill, full in (("g", wg, lambda: fill_a("gate", j, i), a_full),
                                                ("u", wu, lambda: fill_b("up", j, i), b_full)):
                        dst = fill()
                        if j == 0 and i % IPP == 0:
                            pe.wait_ge(rounded, quant_at((kind, i // IPP), KC - 1) + 1)
                        terms = []
                        for k in range(KC):
                            wk = w[:, k, i * P:(i + 1) * P]
                            terms += [(wk, xt_hi[:, j % 2, k, :]), (wk, xt_lo[:, j % 2, k, :])]
                        products(dst[:, :], terms).then_inc(full, 1)
                    if 1 <= j < NCH - 1 and 5 <= i < 5 + TPC:
                        transposes((j + 1) * TPC + i - 5)

            def token_bank(kind, j, t):
                assert TPC == NB and at_b(kind, j, 0) % NB == 0
                return banks_b[:, bass.ds(t, 1), :].rearrange("p a e -> p (a e)")

            def down_first():
                pe.wait_ge(fu_lo_ready, IB)
                pe.wait_ge(fu_hi_ready, IB)
                for n in range(NPI):
                    pe.wait_ge(wd_ready, n + 1)
                    for t in range(TPC):
                        dst = fill_b("down", 0, t)
                        c = t * P
                        terms = []
                        for i in range(n * IPP, (n + 1) * IPP):
                            terms += [(fu_hi[:, i, c:c + P], wd[:, i, :]), (fu_lo[:, i, c:c + P], wd[:, i, :])]
                        last = products(dst[:, :], terms, n == 0, n == NPI - 1)
                        if n == NPI - 1:
                            last.then_inc(b_full, 1)

            def down(j):
                pe.wait_ge(fu_lo_ready, IB * (j + 1))
                pe.wait_ge(fu_hi_ready, IB * (j + 1))
                with pe.Fori(0, TPC) as t:
                    pe.wait_ge(fuse_ready, t + (IB * (j + 1) - NB + 1))
                    tile = bass.ds(t * P, P)
                    terms = []
                    for i in range(IB):
                        terms += [(fu_hi[:, i, tile], wd[:, i, :]), (fu_lo[:, i, tile], wd[:, i, :])]
                    products(token_bank("down", j, t), terms).then_inc(b_full, 1)

            def sum_tokens(b):
                dst = fill_a("asum", 2 * b, 0)
                pe.wait_ge(kv_added, TPB * (b + 1))
                pe.wait_ge(consts_ready, 2)
                for m in range(KC):
                    last = pe.matmul(dst[:, m:m + 1], kv_sum[:, m * P:(m + 1) * P], ones[:, :], start=True, stop=True)
                last.then_inc(a_full, 1)

            def queries(j):
                if j == 0:
                    wait_converted(pe, ("q", 0))
                for m in range(KC):
                    dst = fill_a("q", j, m)
                    terms = []
                    for k in range(KC):
                        hi, lo = wi_hi[:, k, m * P:(m + 1) * P], wi_lo[:, k, m * P:(m + 1) * P]
                        terms += [(hi, xt_hi[:, j % 2, k, :]), (hi, xt_lo[:, j % 2, k, :]), (lo, xt_hi[:, j % 2, k, :])]
                    products(dst[:, :], terms).then_inc(a_full, 1)

            def output(j):
                if j == 0:
                    wait_converted(pe, ("o", 0))
                pe.wait_ge(y_lo_ready, KC * (j + 1))
                pe.wait_ge(y_hi_ready, KC * (j + 1))
                with pe.Fori(0, TPC) as t:
                    pe.wait_ge(down_ready, t + (TPC * j + 1))
                    tile = bass.ds(t * P, P)
                    terms = []
                    for m in (2, 3, 0, 1):
                        hi, lo = y_hi[:, m, tile], y_lo[:, m, tile]
                        terms += [(hi, wo_hi[:, m, :]), (hi, wo_lo[:, m, :]), (lo, wo_hi[:, m, :])]
                    products(token_bank("out", j, t), terms).then_inc(b_full, 1)

            for t in range(TPC):
                transposes(t)
            for j in range(NCH):
                if j == 0:
                    for t in range(TPB):
                        kv_tile(t)
                        if 2 <= t < 2 + TPC:
                            transposes(TPC + t - 2)
                elif j == 2:
                    for t in range(j * TPC, (j + 1) * TPC):
                        kv_tile(t)
                gate_up(j)
                if j == 2:
                    for t in range((j + 1) * TPC, (j + 2) * TPC):
                        kv_tile(t)
                queries(j)
                if j % 2 == 0:
                    sum_tokens(j // 2)
                if j == 0:
                    down_first()
                else:
                    down(j)
                output(j)


def rotation_tables():
    inv_freq = (1.0 / (10000.0 ** (np.arange(0, ROT, 2, dtype=np.float64) / ROT))).astype(np.float32)
    angle = (np.arange(S, dtype=np.float32)[:, None] * inv_freq[None, :]).astype(np.float64)
    return np.cos(angle).astype(np.float32), np.sin(angle).astype(np.float32)


def kernel(L0_attn_X, L0_attn_W_in, L0_attn_b_in, L0_attn_W_out, L0_attn_b_out, L0_ffn_gate_w, L0_ffn_up_w,
           L0_ffn_down_w, L0_ffn_gate_scale, L0_ffn_up_scale, L0_ffn_down_scale):
    import concourse.bacc as bacc
    from concourse.bass_utils import run_bass_kernel_spmd

    c = np.ascontiguousarray
    order = np.concatenate([np.arange(0, ROT, 2), np.arange(1, ROT, 2), np.arange(ROT, D)])
    order3 = np.concatenate([order, D + order, 2 * D + order])
    b_in = np.asarray(L0_attn_b_in)[order3]
    cos, sin = rotation_tables()
    arrays = {
        "x": c(np.asarray(L0_attn_X).reshape(B * S, D)),
        "w_in_t": c(np.asarray(L0_attn_W_in)[order3].T),
        "b_qc": c(b_in[0:D].reshape(KC, P).T),
        "b_k": c(b_in[D:2 * D]),
        "b_v": c(b_in[2 * D:3 * D]),
        "w_out_t": c(np.asarray(L0_attn_W_out).T[order]),
        "b_out": c(np.asarray(L0_attn_b_out)),
        "gate_w": c(np.asarray(L0_ffn_gate_w)),
        "up_w": c(np.asarray(L0_ffn_up_w)),
        "down_w": c(np.asarray(L0_ffn_down_w)),
        "gate_s": c(np.asarray(L0_ffn_gate_scale).reshape(IB, P).T),
        "up_s": c(np.asarray(L0_ffn_up_scale).reshape(IB, P).T),
        "down_s": c(np.asarray(L0_ffn_down_scale)),
        "cos_f": c(cos.T),
        "sin_f": c(sin.T),
        "cos_t": c(cos.reshape(TPB, P, HALF).transpose(1, 0, 2)),
        "sin_t": c(sin.reshape(TPB, P, HALF).transpose(1, 0, 2)),
    }
    nc = bacc.Bacc("TRN2", target_bir_lowering=False, num_devices=1)
    args = [nc.dram_tensor(n, a.shape, mybir.dt.from_np(a.dtype), kind="ExternalInput").ap() for n, a in arrays.items()]
    args.append(nc.dram_tensor("out", (B * S, D), F32, kind="ExternalOutput").ap())
    build(nc, *args)
    r = run_bass_kernel_spmd(nc, [arrays], core_ids=[0])
    return r.results[0]["out"].reshape(B, S, D)
```
